# Optimizing a Trainium2 kernel written in Bass

```python
import numpy as np
import jax
import jax.numpy as jnp

def _softmax(x, axis=-1):
    return jax.nn.softmax(x, axis=axis)

def _gelu(x):
    return jax.nn.gelu(x, approximate=True)

def _silu(x):
    return jax.nn.silu(x)

def _sigmoid(x):
    return jax.nn.sigmoid(x)

def _layernorm(x, axis=-1, eps=1e-05):
    m = jnp.mean(x, axis=axis, keepdims=True)
    v = jnp.var(x, axis=axis, keepdims=True)
    return (x - m) / jnp.sqrt(v + eps)

def _scatter_add(tgt, idx, src, axis=0):
    return tgt.at[idx].add(src)

def _segment_sum(src, seg, n):
    return jax.ops.segment_sum(src, seg, n)
kernel_name = 'mk_flamingo_gated_d1_seqx_r8_fb9070'

def setup_inputs(seed: int=0):
    np.random.seed(seed)
    _w = jnp.asarray

    def _rec_inputs():
        import jax
        import jax.numpy as jnp
        _rk = jax.random.key(seed)
        x = 0.002226 + 0.9996 * jax.random.normal(jax.random.fold_in(_rk, 1), (128, 64, 128), jnp.float32)
        _lenS = 64 - jax.random.randint(jax.random.fold_in(_rk, 7), (128,), 0, max(1, 64 // 4) + 1, jnp.int32)
        _lenS2 = 64 - jax.random.randint(jax.random.fold_in(_rk, 8), (128,), 0, max(1, 64 // 4) + 1, jnp.int32)
        _ctx_1024P = jax.random.normal(jax.random.fold_in(_rk, 11), (128, 16, 128), jnp.float32)
        _ctx_1024c = jax.random.dirichlet(jax.random.fold_in(_rk, 511), 0.3 * jnp.ones((16,), jnp.float32), (128, 64))
        _ctx_1024t = jnp.einsum('bsk,bkd->bsd', _ctx_1024c, _ctx_1024P)
        _ctx_1024t = _ctx_1024t * jax.lax.rsqrt(jnp.mean(jnp.square(_ctx_1024t)) + 1e-12) * 0.953939
        ctx_1024 = -0.000125008 + 0.999885 * (_ctx_1024t + 0.3 * jax.random.normal(jax.random.fold_in(_rk, 611), (128, 64, 128), jnp.float32))
        _g = jax.random.normal(jax.random.fold_in(_rk, 9001), (2, 1), jnp.float32)
        _g = jnp.sign(_g) * jnp.maximum(jnp.abs(_g), 1.0) + (_g == 0) * 1.0
        g_xattn = _g[0]
        g_ffn = _g[1]
        return (x, ctx_1024, g_xattn, g_ffn)
    x, ctx_1024, g_xattn, g_ffn = _rec_inputs()

    def _L0_xattn_setup():
        import jax, jax.numpy as jnp
        import numpy as np
        B, M, N, DIM, DH, H = (8, 512, 64, 128, 128, 8)
        INNER = DH * H
        EPS = 1e-05

        def _layernorm(x, g, b):
            mu = jnp.mean(x, axis=-1, keepdims=True)
            var = jnp.var(x, axis=-1, keepdims=True)
            return (x - mu) * jax.lax.rsqrt(var + EPS) * g + b
        key = jax.random.key(seed)
        ks = jax.random.split(key, 8)
        sd = 0.02
        return {'x': jax.random.normal(ks[0], (B, M, DIM), jnp.float32), 'latents': jax.random.normal(ks[1], (B, N, DIM), jnp.float32), 'gamma_media': jnp.ones((DIM,), jnp.float32), 'beta_media': jnp.zeros((DIM,), jnp.float32), 'gamma_lat': jnp.ones((DIM,), jnp.float32), 'beta_lat': jnp.zeros((DIM,), jnp.float32), 'Wq': jax.random.normal(ks[2], (DIM, INNER), jnp.float32) * sd, 'bq': jnp.zeros((INNER,), jnp.float32), 'Wkv': jax.random.normal(ks[3], (DIM, 2 * INNER), jnp.float32) * sd, 'bkv': jnp.zeros((2 * INNER,), jnp.float32), 'Wo': jax.random.normal(ks[4], (INNER, DIM), jnp.float32) * sd, 'bo': jnp.zeros((DIM,), jnp.float32)}
    _L0_xattn_all = _L0_xattn_setup()
    _L0_xattn_in = {k: v for k, v in _L0_xattn_all.items() if k in ('gamma_media', 'beta_media', 'gamma_lat', 'beta_lat', 'Wq', 'bq', 'Wkv', 'bkv', 'Wo', 'bo')}
    del _L0_xattn_all

    def _L0_ffn_setup():
        import jax, jax.numpy as jnp
        import numpy as np
        B, S, H, E, K = (2, 128, 128, 8, 2)
        D = 2 * H
        key = jax.random.key(seed)
        ks = jax.random.split(key, 7)
        x = jax.random.normal(ks[0], (B, S, H), dtype=jnp.float32)
        Wr = jax.random.normal(ks[1], (H, E), dtype=jnp.float32) / np.sqrt(H)
        br = jnp.zeros((E,), dtype=jnp.float32)
        W1 = jax.random.normal(ks[2], (E, H, D), dtype=jnp.float32) / np.sqrt(H)
        b1 = jnp.zeros((E, D), dtype=jnp.float32)
        W2 = jax.random.normal(ks[3], (E, D, H), dtype=jnp.float32) / np.sqrt(D)
        b2 = jnp.zeros((E, H), dtype=jnp.float32)
        return {'x': x, 'Wr': Wr, 'br': br, 'W1': W1, 'b1': b1, 'W2': W2, 'b2': b2}
    _L0_ffn_all = _L0_ffn_setup()
    _L0_ffn_in = {k: v for k, v in _L0_ffn_all.items() if k in ('Wr', 'br', 'W1', 'b1', 'W2', 'b2')}
    del _L0_ffn_all
    return {'x': x, 'ctx_1024': ctx_1024, 'g_xattn': g_xattn, 'g_ffn': g_ffn, 'L0_xattn_gamma_media': _L0_xattn_in['gamma_media'], 'L0_xattn_beta_media': _L0_xattn_in['beta_media'], 'L0_xattn_gamma_lat': _L0_xattn_in['gamma_lat'], 'L0_xattn_beta_lat': _L0_xattn_in['beta_lat'], 'L0_xattn_Wq': _L0_xattn_in['Wq'], 'L0_xattn_bq': _L0_xattn_in['bq'], 'L0_xattn_Wkv': _L0_xattn_in['Wkv'], 'L0_xattn_bkv': _L0_xattn_in['bkv'], 'L0_xattn_Wo': _L0_xattn_in['Wo'], 'L0_xattn_bo': _L0_xattn_in['bo'], 'L0_ffn_Wr': _L0_ffn_in['Wr'], 'L0_ffn_br': _L0_ffn_in['br'], 'L0_ffn_W1': _L0_ffn_in['W1'], 'L0_ffn_b1': _L0_ffn_in['b1'], 'L0_ffn_W2': _L0_ffn_in['W2'], 'L0_ffn_b2': _L0_ffn_in['b2']}

def reference(x, ctx_1024, g_xattn, g_ffn, L0_xattn_gamma_media, L0_xattn_beta_media, L0_xattn_gamma_lat, L0_xattn_beta_lat, L0_xattn_Wq, L0_xattn_bq, L0_xattn_Wkv, L0_xattn_bkv, L0_xattn_Wo, L0_xattn_bo, L0_ffn_Wr, L0_ffn_br, L0_ffn_W1, L0_ffn_b1, L0_ffn_W2, L0_ffn_b2):
    import jax
    import jax.numpy as jnp

    def _L0_xattn_ref(x, latents, gamma_media, beta_media, gamma_lat, beta_lat, Wq, bq, Wkv, bkv, Wo, bo):
        import jax, jax.numpy as jnp
        import numpy as np
        B, M, N, DIM, DH, H = (8, 512, 64, 128, 128, 8)
        INNER = DH * H
        EPS = 1e-05

        def _layernorm(x, g, b):
            mu = jnp.mean(x, axis=-1, keepdims=True)
            var = jnp.var(x, axis=-1, keepdims=True)
            return (x - mu) * jax.lax.rsqrt(var + EPS) * g + b
        b = x.shape[0]
        xn = _layernorm(x, gamma_media, beta_media)
        ln = _layernorm(latents, gamma_lat, beta_lat)
        q = ln @ Wq + bq
        kv_input = jnp.concatenate([xn, ln], axis=1)
        kv = kv_input @ Wkv + bkv
        k, v = jnp.split(kv, 2, axis=-1)

        def to_heads(t):
            return t.reshape(b, t.shape[1], H, DH).transpose(0, 2, 1, 3)
        q, k, v = (to_heads(q), to_heads(k), to_heads(v))
        q = q * DH ** (-0.5)
        sim = jnp.einsum('bhid,bhjd->bhij', q, k)
        attn = jax.nn.softmax(sim, axis=-1)
        out = jnp.einsum('bhij,bhjd->bhid', attn, v)
        out = out.transpose(0, 2, 1, 3).reshape(b, -1, INNER)
        return out @ Wo + bo

    def _L0_ffn_ref(x, Wr, br, W1, b1, W2, b2):
        import jax, jax.numpy as jnp
        import numpy as np
        B, S, H, E, K = (2, 128, 128, 8, 2)
        D = 2 * H
        logits = jnp.einsum('bsh,he->bse', x, Wr) + br
        probs = jax.nn.softmax(logits, axis=-1)
        top_p, top_i = jax.lax.top_k(probs, K)
        cw = jnp.sum(jax.nn.one_hot(top_i, E, dtype=x.dtype) * top_p[..., None], axis=-2)
        h = jax.nn.relu(jnp.einsum('bsh,ehd->bsed', x, W1) + b1)
        y = jnp.einsum('bsed,edh->bseh', h, W2) + b2
        out = jnp.einsum('bseh,bse->bsh', y, cw)
        return out
    x = x + jnp.tanh(g_xattn[0]) * _L0_xattn_ref(ctx_1024, _layernorm(x, axis=-1), L0_xattn_gamma_media, L0_xattn_beta_media, L0_xattn_gamma_lat, L0_xattn_beta_lat, L0_xattn_Wq, L0_xattn_bq, L0_xattn_Wkv, L0_xattn_bkv, L0_xattn_Wo, L0_xattn_bo)
    x = x + jnp.tanh(g_ffn[0]) * _L0_ffn_ref(_layernorm(x, axis=-1), L0_ffn_Wr, L0_ffn_br, L0_ffn_W1, L0_ffn_b1, L0_ffn_W2, L0_ffn_b2)
    return x

_drawn_inputs = setup_inputs


def setup_inputs(seed=0):
    import zlib

    import numpy as np

    out = dict(_drawn_inputs(seed))
    spreads = {'L0_xattn_gamma_media': (1.0, 0.6),
     'L0_xattn_beta_media': (0.0, 0.559),
     'L0_xattn_gamma_lat': (1.0, 0.6),
     'L0_xattn_beta_lat': (0.0, 0.446),
     'L0_xattn_bq': (0.0, 2.0),
     'L0_xattn_bkv': (0.0, 0.1),
     'L0_xattn_bo': (0.0, 0.1),
     'L0_ffn_br': (0.0, 0.1),
     'L0_ffn_b1': (0.0, 0.289),
     'L0_ffn_b2': (0.0, 0.1)}
    factors = {'L0_xattn_Wq': 8.0}
    for name, (base, spread) in spreads.items():
        noise = np.random.default_rng([zlib.crc32(name.encode()), seed]).standard_normal(out[name].shape)
        drawn = base * np.exp(spread * noise) if base else spread * noise
        out[name] = jnp.asarray(drawn.astype(out[name].dtype))
    for name, factor in factors.items():
        out[name] = (out[name] * factor).astype(out[name].dtype)
    return out
```

```python
from contextlib import ExitStack

import concourse.bass as bass
from concourse import mybir

F32 = mybir.dt.float32
F32R = mybir.dt.float32r
ALU = mybir.AluOpType
ACT = mybir.ActivationFunctionType
AX = mybir.AxisListType.X

P = 128
D = 128
B = 128
L = 64
H = 8
E = 8
GB = 8
G = B // GB
TOK = GB * L
EPS = 1e-5
SCALE = float(D) ** -0.5

LOAD, STATS, CENTER, AFFINE = -12, -11, -10, -9
SPLIT = -7
FFN = 15
FIRST, LAST = LOAD, GB * (G - 1) + 25
PER_TRIP = 2 * GB
LOOP_AT, TRIPS = 32, 5

SHARED = {
    0: [("turn_kv", 1)],
    1: [("turn_kv", 1), ("finish", -3), ("project", -1)],
    2: [("turn_kv", 1), ("residual", -1)],
    3: [("turn_kv", 1)],
    4: [("query", 1), ("turn_x", -1), ("query", 1)],
    5: [("query", 1), ("router", -1), ("query", 1)],
    6: [("query", 1), ("turn_cw", -1), ("query", 1)],
    7: [("query", 1), ("query", 1)],
}


def plan_shared():
    uses, used = {}, [0, 0]
    for n in range(FIRST, LAST + 1):
        g, s = n // GB, n % GB
        at = sum(len(SHARED[t]) for t in range(s))
        uses[n] = []
        heads = 0
        for what, off in SHARED[s]:
            bank, at = at % 2, at + 1
            sub = 2 * (s - 4) + heads if what == "query" else s
            heads += what == "query"
            if 0 <= g + off < G:
                uses[n].append((what, g + off, sub, bank, used[bank]))
                used[bank] += 1
    return uses


def flamingo(nc, x, ctx_in, g_xattn, g_ffn, gamma_m, beta_m, gamma_l, beta_l, Wq, bq, Wkv, bkv, Wo, bo,
             Wr, br, W1, b1, W2, b2, out):
    uses = plan_shared()
    use_at = {(what, g, sub): (bank, before) for n in uses for what, g, sub, bank, before in uses[n]}
    shared_per_trip = sum(len(v) for v in SHARED.values())

    ctx = ExitStack()
    with ctx:
        def sb(name, shape, dt=F32):
            return ctx.enter_context(nc.sbuf_tensor(name, shape, dt))

        def psum(name):
            return ctx.enter_context(nc.psum_tensor(name, [P, 512], F32))

        def sem(name):
            return ctx.enter_context(nc.semaphore(name))

        kv = sb("kv", [P, GB, D])
        kv_hi = sb("kv_hi", [P, 2, GB, D], F32R)
        kv_lo = sb("kv_lo", [P, 2, GB, D], F32R)
        kvT_hi = sb("kvT_hi", [P, 2, GB, P], F32R)
        kvT_lo = sb("kvT_lo", [P, 2, GB, P], F32R)
        qT_hi = sb("qT_hi", [P, 2, GB, H, L], F32R)
        qT_lo = sb("qT_lo", [P, 2, GB, H, L], F32R)
        probs = sb("probs", [P, 2, 512])
        pT_hi = sb("pT_hi", [P, 512], F32R)
        pT_lo = sb("pT_lo", [P, 512], F32R)
        oT = sb("oT", [P, H, TOK])
        yT = sb("yT", [P, TOK])
        xres = sb("xres", [P, 4, D])
        x1 = sb("x1", [P, 2, 4, D])
        xn = sb("xn", [P, 4, D])
        xT_hi = sb("xT_hi", [P, 2, TOK], F32R)
        xT_lo = sb("xT_lo", [P, 2, TOK], F32R)
        cwT = sb("cwT", [E, TOK])
        cw_all = sb("cw_all", [P, 2, TOK])
        hs = sb("hs", [P, 2, 2, TOK])
        hr = sb("hr", [P, TOK])
        fT = sb("fT", [P, TOK])
        res = sb("res", [P, 4, D])
        A_hi = sb("A_hi", [P, H, D], F32R)
        A_lo = sb("A_lo", [P, H, D], F32R)
        M = sb("M", [P, H, D])
        W1_hi = sb("W1_hi", [P, E, 2, P], F32R)
        W1_lo = sb("W1_lo", [P, E, 2, P], F32R)
        W2_sb = sb("W2_sb", [P, E, 2, D])
        Wr_f = sb("Wr_f", [P, E])
        Wr_hi = sb("Wr_hi", [P, E], F32R)
        Wr_lo = sb("Wr_lo", [P, E], F32R)
        NR = 2 * H + 2 * E + 1
        rows = sb("rows", [NR, D])
        cols = sb("cols", [P, NR])
        tb = sb("tb", [P, H])
        neg_b1 = sb("neg_b1", [P, 2 * E])
        b1_diag = sb("b1_diag", [P, E, E])
        b2_f = sb("b2_f", [E, D])
        B2 = sb("B2", [E, D])
        gamma = sb("gamma", [P, D])
        beta = sb("beta", [P, D])
        br_all = sb("br_all", [P, E])
        gates = sb("gates", [P, 2])
        tg = sb("tg", [P, 2])
        bo_sum = sb("bo_sum", [P, 1])
        tg_bo = sb("tg_bo", [P, 1])
        ident = sb("ident", [P, P])
        ones_sq = sb("ones_sq", [P, P])
        before = sb("before", [P, E, E])
        neg_half = sb("neg_half", [P, GB])
        eps = sb("eps", [P, GB])
        exponent = sb("exponent", [P, GB])
        stats = sb("stats", [P, GB, 6])
        mv = sb("mv", [P, GB, 2])
        rstd = sb("rstd", [P, GB])
        var_eps = sb("var_eps", [P, GB])
        rstd2 = sb("rstd2", [P, GB])
        neg_max = sb("neg_max", [P, 2, 4])
        sums = sb("sums", [P, 2, 4])
        rsums = sb("rsums", [P, 2, 4])
        stats1 = sb("stats1", [P, 4, 6])
        mv1 = sb("mv1", [P, 4, 2])
        var_eps1 = sb("var_eps1", [P, 4])
        rstd1 = sb("rstd1", [P, 4])
        logit = sb("logit", [P, 4, E])
        shift = sb("shift", [P, 4, E])
        prob = sb("prob", [P, 4, E])
        probn = sb("probn", [P, 4, E])
        top = sb("top", [P, 4])
        psumr = sb("psumr", [P, 4])
        prec = sb("prec", [P, 4])
        gt = sb("gt", [P, 4, E, E])
        eq = sb("eq", [P, 4, E, E])
        eqb = sb("eqb", [P, 4, E, E])
        rank = sb("rank", [P, 4, E])
        cw = sb("cw", [P, 4, E])
        Wq_in = oT[:, 0:2, :].rearrange("p a n -> p (a n)")
        Wkv_in = oT[:, 2:6, :].rearrange("p a n -> p (a n)")
        Wo_in = oT[:, 6:8, :].rearrange("p a n -> p (a n)").rearrange("p (h n) -> p h n", h=H)
        W1_in = hs[:, :, :, :].rearrange("p a c (k f) -> p (a c k) f", f=P)
        wT = probs

        scores = psum("scores")
        pT = psum("pT")
        o = psum("o")
        hid = [psum("hid0"), psum("hid1")]
        acc = psum("acc")
        shared = [psum("shared0"), psum("shared1")]

        cw_dram = nc.dram_tensor("cw_rows", (2, E, TOK), F32).ap()

        got_rows = sem("got_rows")
        got_attn_w = sem("got_attn_w")
        got_ffn_w = sem("got_ffn_w")
        got_small = sem("got_small")
        got_kv = sem("got_kv")
        got_xres = sem("got_xres")
        const_step = sem("const_step")
        gates_done = sem("gates_done")
        cols_turned = sem("cols_turned")
        cols_ready = sem("cols_ready")
        w_turned = sem("w_turned")
        w_copied = sem("w_copied")
        w_folded = sem("w_folded")
        w_hi = sem("w_hi")
        w_out = sem("w_out")
        bias_folded = sem("bias_folded")
        bias_ready = sem("bias_ready")
        diag_ready = sem("diag_ready")
        ffn_hi = sem("ffn_hi")
        ffn_ready = sem("ffn_ready")
        stats_done = sem("stats_done")
        mv_done = sem("mv_done")
        rstd_step = sem("rstd_step")
        kv_centered = sem("kv_centered")
        kv_affine = sem("kv_affine")
        kv_hi_done = sem("kv_hi_done")
        kv_lo_done = sem("kv_lo_done")
        scores_ready = sem("scores_ready")
        max_ready = sem("max_ready")
        exp_done = sem("exp_done")
        rsum_ready = sem("rsum_ready")
        probs_ready = sem("probs_ready")
        pT_ready = sem("pT_ready")
        pT_hi_done = sem("pT_hi_done")
        pT_lo_done = sem("pT_lo_done")
        o_ready = sem("o_ready")
        o_out = sem("o_out")
        stats1_done = sem("stats1_done")
        mv1_done = sem("mv1_done")
        rstd1_step = sem("rstd1_step")
        xn_done = sem("xn_done")
        router_step = sem("router_step")
        rexp_done = sem("rexp_done")
        cw_stored = sem("cw_stored")
        got_cw = [sem("got_cw_even"), sem("got_cw_odd")]
        hid0_ready = sem("hid0_ready")
        hid1_ready = sem("hid1_ready")
        hs0_done = sem("hs0_done")
        relu_done = sem("relu_done")
        hs1_done = sem("hs1_done")
        ffn_done = sem("ffn_done")
        f_done = sem("f_done")
        stored = sem("stored")
        shared_full = [sem("shared_full0"), sem("shared_full1")]
        shared_out = [sem("shared_out0"), sem("shared_out1")]
        kvT_hi_done = sem("kvT_hi_done")
        q_hi_done = sem("q_hi_done")
        xT_hi_done = sem("xT_hi_done")

        def slots(eng, body):
            for n in range(FIRST, LOOP_AT):
                body(n, 0)
            with eng.Fori(0, TRIPS) as trip:
                for n in range(LOOP_AT, LOOP_AT + PER_TRIP):
                    body(n, trip)
            for n in range(LOOP_AT + PER_TRIP * TRIPS, LAST + 1):
                body(n, 0)

        def wait(eng, s, value, per_slot, trip):
            if value > 0:
                eng.wait_ge(s, value + trip * int(per_slot * PER_TRIP))

        def wait_shared(eng, sems, what, g, sub, trip):
            if (what, g, sub) in use_at:
                bank, count = use_at[what, g, sub]
                eng.wait_ge(sems[bank], count + 1 + trip * shared_per_trip)

        def count_in_register(eng, value, per_slot, trip):
            if not isinstance(trip, int):
                eng.compute_val(value + trip * int(per_slot * PER_TRIP))

        def first_row(eng, g, trip):
            return g * GB if isinstance(trip, int) else eng.snap((g + 2 * trip) * GB)

        def expert_of(n):
            f = n - FFN
            return f if 0 <= f < G * E else None

        block = ctx.enter_context(nc.Block())

        @block.sync
        def _(sp):
            sp.dma_start(rows[0:H, :], bq.rearrange("(h d) -> h d", h=H)).then_inc(got_rows, 16)
            sp.dma_start(rows[H:2 * H, :], bkv[H * D:2 * H * D].rearrange("(h d) -> h d", h=H)).then_inc(got_rows, 16)
            sp.dma_start(rows[2 * H:2 * H + 2 * E, :], b1.rearrange("e (c f) -> (e c) f", c=2)).then_inc(got_rows, 16)
            sp.dma_start(rows[NR - 1:NR, :], bo.rearrange("(a n) -> a n", a=1)).then_inc(got_rows, 16)
            sp.dma_start(Wq_in, Wq).then_inc(got_attn_w, 16)
            sp.dma_start(Wkv_in, Wkv).then_inc(got_attn_w, 16)
            sp.dma_start(Wo_in, Wo.rearrange("(h e) n -> e h n", h=H)).then_inc(got_attn_w, 16)

            def slot(n, trip):
                s = n % GB
                g = (n - LOAD) // GB
                if s == LOAD % GB and 0 <= g < G:
                    at = bass.ds(first_row(sp, g, trip), GB)
                    count_in_register(sp, 4 * g, 4 / GB, trip)
                    count_in_register(sp, g, 1 / GB, trip)
                    wait(sp, kvT_hi_done, 4 * g, 4 / GB, trip)
                    wait(sp, kv_hi_done, g, 1 / GB, trip)
                    wait(sp, kv_lo_done, g, 1 / GB, trip)
                    sp.dma_start(kv[0:L, :, :], ctx_in[at, :, :].rearrange("b s d -> s b d")).then_inc(got_kv, 16)
                    sp.dma_start(kv[L:P, :, :], x[at, :, :].rearrange("b s d -> s b d")).then_inc(got_kv, 16)
                g = n // GB
                if s == 4 and 0 <= g < G:
                    at = bass.ds(first_row(sp, g, trip), GB)
                    wait_shared(sp, shared_out, "residual", g - 1, 2, trip)
                    sp.dma_start(xres[:, :, :], x[at, :, :].rearrange("(c b) s d -> (b s) c d", b=2)).then_inc(got_xres, 16)
                g = n // GB - 1
                if s == 6 and 0 <= g < G:
                    count_in_register(sp, 8 * E * (g - 1), 8, trip)
                    wait_shared(sp, shared_out, "turn_cw", g, 6, trip)
                    wait(sp, got_cw[0], 8 * E * (g - 1), 8, trip)
                    wait(sp, got_cw[1], 8 * E * (g - 1), 8, trip)
                    sp.dma_start(cw_dram[g % 2, :, :], cwT[:, :]).then_inc(cw_stored, 16)
                f = expert_of(n + 1)
                if f is not None:
                    stored_count, used_count = 16 * (f // E + 1) + trip * 32, f - 1 + trip * PER_TRIP
                    count_in_register(sp, 16 * (f // E + 1), 16 / GB, trip)
                    count_in_register(sp, f - 1, 1, trip)
                    sp.wait_ge(cw_stored, stored_count)
                    if f > 1:
                        sp.wait_ge(hs0_done, used_count)
                        sp.wait_ge(hs1_done, used_count)
                    sp.dma_start(cw_all[:, f % 2, :],
                                 cw_dram[f // E % 2, f % E, :].partition_broadcast(P)).then_inc(got_cw[f % 2], 16)
                g = n // GB - 3
                if s == 1 and 0 <= g < G:
                    at = bass.ds(first_row(sp, g, trip), GB)
                    wait_shared(sp, shared_out, "finish", g, 1, trip)
                    sp.dma_start(out[at, :, :].rearrange("(c b) s d -> (b s) c d", b=2), res[:, :, :]).then_inc(stored, 16)

            slots(sp, slot)
            sp.wait_ge(stored, 16 * G)
            sp.wait_ge(cw_stored, 16 * G)

        @block.gpsimd
        def _(pool):
            nc.gpsimd.memset(neg_half[:, :], -0.5).then_inc(const_step, 1)
            pool.wait_ge(const_step, 1)
            nc.gpsimd.affine_select(out=exponent[:, :], in_=neg_half[:, :], compare_op=ALU.is_ge, fill=0.0,
                                    base=-L, pattern=[[0, GB]], channel_multiplier=1).then_inc(const_step, 1)
            nc.gpsimd.memset(eps[:, :], EPS).then_inc(const_step, 1)
            nc.gpsimd.memset(ones_sq[:, :], 1.0).then_inc(const_step, 1)
            nc.gpsimd.memset(b1_diag[:, :, :], 0.0).then_inc(const_step, 1)
            nc.gpsimd.memset(eq[:, 0, :, :], 1.0).then_inc(const_step, 1)
            pool.wait_ge(const_step, 6)
            nc.gpsimd.affine_select(out=ident[:, :], in_=ones_sq[:, :], compare_op=ALU.is_equal, fill=0.0,
                                    base=0, pattern=[[-1, P]], channel_multiplier=1).then_inc(const_step, 1)
            nc.gpsimd.affine_select(out=before[:, :, :], in_=eq[:, 0, :, :], compare_op=ALU.is_gt, fill=0.0,
                                    base=0, pattern=[[1, E], [-1, E]], channel_multiplier=0).then_inc(const_step, 1)
            pool.wait_ge(got_small, 16 * 8)

            def slot(n, trip):
                s = n % GB
                if 0 <= n < B:
                    wait(pool, rsum_ready, n + 1, 1, trip)
                    pv = probs[:, n % 2, :].rearrange("p (c j) -> p c j", c=4)
                    nc.gpsimd.tensor_tensor(pv, pv, rsums[:, n % 2, :].unsqueeze(2).broadcast_to([P, 4, P]),
                                            ALU.mult).then_inc(probs_ready, 1)
                g = (n - STATS) // GB
                if s == STATS % GB and 0 <= g < G:
                    at = 7 * g
                    wait(pool, mv_done, g + 1, 1 / GB, trip)
                    wait(pool, rstd_step, at, 7 / GB, trip)
                    nc.gpsimd.tensor_tensor(var_eps[:, :], mv[:, :, 1], eps[:, :], ALU.add).then_inc(rstd_step, 1)
                    wait(pool, rstd_step, at + 1, 7 / GB, trip)
                    nc.gpsimd.tensor_tensor(rstd[:, :], var_eps[:, :], neg_half[:, :], ALU.pow).then_inc(rstd_step, 1)
                    wait(pool, rstd_step, at + 2, 7 / GB, trip)
                    nc.gpsimd.tensor_tensor(var_eps[:, :], mv[:, :, 1], rstd[:, :], ALU.mult).then_inc(rstd_step, 1)
                    wait(pool, rstd_step, at + 3, 7 / GB, trip)
                    nc.gpsimd.tensor_tensor(var_eps[:, :], var_eps[:, :], rstd[:, :], ALU.mult).then_inc(rstd_step, 1)
                    wait(pool, rstd_step, at + 4, 7 / GB, trip)
                    nc.gpsimd.tensor_tensor(var_eps[:, :], var_eps[:, :], eps[:, :], ALU.add).then_inc(rstd_step, 1)
                    wait(pool, rstd_step, at + 5, 7 / GB, trip)
                    nc.gpsimd.tensor_tensor(rstd2[:, :], var_eps[:, :], exponent[:, :], ALU.pow).then_inc(rstd_step, 1)
                    wait(pool, rstd_step, at + 6, 7 / GB, trip)
                    nc.gpsimd.tensor_tensor(rstd[:, :], rstd[:, :], rstd2[:, :], ALU.mult).then_inc(rstd_step, 1)
                g = (n - AFFINE) // GB
                if s == AFFINE % GB and 0 <= g < G:
                    wait(pool, kv_centered, g + 1, 1 / GB, trip)
                    nc.gpsimd.tensor_tensor(kv[:, :, :], kv[:, :, :], gamma[:, :].unsqueeze(1).broadcast_to([P, GB, D]),
                                            ALU.mult).then_inc(kv_affine, 1)
                    wait(pool, kv_affine, 2 * g + 1, 2 / GB, trip)
                    nc.gpsimd.tensor_tensor(kv[:, :, :], kv[:, :, :], beta[:, :].unsqueeze(1).broadcast_to([P, GB, D]),
                                            ALU.add).then_inc(kv_affine, 1)
                g = n // GB - 1
                if s == 3 and 0 <= g < G:
                    wait(pool, mv1_done, g + 1, 1 / GB, trip)
                    wait(pool, rstd1_step, 2 * g, 2 / GB, trip)
                    nc.gpsimd.tensor_tensor(var_eps1[:, :], mv1[:, :, 1], eps[:, 0:4], ALU.add).then_inc(rstd1_step, 1)
                    wait(pool, rstd1_step, 2 * g + 1, 2 / GB, trip)
                    nc.gpsimd.tensor_tensor(rstd1[:, :], var_eps1[:, :], neg_half[:, 0:4], ALU.pow).then_inc(rstd1_step, 1)
                f = expert_of(n)
                if f is not None:
                    wait(pool, relu_done, f + 1, 1, trip)
                    wait(pool, got_cw[f % 2], 16 * (f // 2 + 1), 8, trip)
                    wait(pool, ffn_done, f - 1, 1, trip)
                    nc.gpsimd.tensor_tensor(hs[:, f % 2, 1, :], hr[:, :], cw_all[:, f % 2, :],
                                            ALU.mult).then_inc(hs1_done, 1)

            slots(pool, slot)

        @block.scalar
        def _(act):
            act.dma_start(gates[:, 0:1], g_xattn.partition_broadcast(P)).then_inc(got_small, 16)
            act.dma_start(gates[:, 1:2], g_ffn.partition_broadcast(P)).then_inc(got_small, 16)
            act.dma_start(gamma[0:L, :], gamma_m.partition_broadcast(L)).then_inc(got_small, 16)
            act.dma_start(gamma[L:P, :], gamma_l.partition_broadcast(L)).then_inc(got_small, 16)
            act.dma_start(beta[0:L, :], beta_m.partition_broadcast(L)).then_inc(got_small, 16)
            act.dma_start(beta[L:P, :], beta_l.partition_broadcast(L)).then_inc(got_small, 16)
            act.dma_start(br_all[:, :], br.partition_broadcast(P)).then_inc(got_small, 16)
            act.dma_start(b2_f[:, :], b2).then_inc(got_small, 16)
            act.dma_start(W1_in.rearrange("p (e c) f -> p e (c f)", c=2), W1.rearrange("e d f -> d e f")).then_inc(got_ffn_w, 16)
            act.dma_start(W2_sb[:, :, :, :], W2.rearrange("e (c f) n -> f e c n", c=2)).then_inc(got_ffn_w, 16)
            act.dma_start(Wr_f[:, :], Wr).then_inc(got_ffn_w, 16)
            act.wait_ge(got_small, 16 * 8)
            nc.scalar.activation(tg[:, :], gates[:, :], ACT.Tanh).then_inc(gates_done, 1)
            act.wait_ge(cols_turned, 1)
            nc.scalar.activation(cols[:, :], shared[0][:, 0:NR], ACT.Copy).then_inc(cols_ready, 1)
            for h in range(H):
                act.wait_ge(w_turned, h + 1)
                if h >= 2:
                    act.wait_ge(w_folded, h - 1)
                nc.scalar.activation(wT[:, h % 2, 0:3 * P], hid[h % 2][:, 0:3 * P], ACT.Copy).then_inc(w_copied, 1)
                act.wait_ge(w_folded, h + 1)
                nc.scalar.activation(A_hi[:, h, :], [pT, o][h % 2][:, 0:D], ACT.Copy, scale=SCALE).then_inc(w_hi, 1)
            act.wait_ge(got_ffn_w, 16 * 3)
            nc.scalar.activation(W1_hi[:, :, :, :].rearrange("p e c f -> p (e c) f"), W1_in, ACT.Copy).then_inc(ffn_hi, 1)
            nc.scalar.activation(Wr_hi[:, :], Wr_f[:, :], ACT.Copy).then_inc(ffn_hi, 1)
            act.wait_ge(bias_ready, 4)

            def slot(n, trip):
                s = n % GB
                g = n // GB - 3
                if s == 0 and 0 <= g < G:
                    wait(act, ffn_done, E * (g + 1), 1, trip)
                    wait_shared(act, shared_full, "finish", g - 1, 1, trip)
                    nc.scalar.activation(fT[:, :], acc[:, :], ACT.Copy).then_inc(f_done, 1)
                m = n - 1
                if 0 <= m < B:
                    wait(act, pT_ready, m + 1, 1, trip)
                    wait(act, o_ready, m, 1, trip)
                    nc.scalar.activation(pT_hi[:, :], pT[:, :], ACT.Copy).then_inc(pT_hi_done, 1)
                if 0 <= n < B:
                    wait(act, max_ready, n + 1, 1, trip)
                    wait(act, pT_ready, n - 1, 1, trip)
                    wait(act, rsum_ready, n - 1, 1, trip)
                    for c in range(4):
                        last = nc.scalar.activation(probs[:, n % 2, c * P:(c + 1) * P], scores[:, c * P:(c + 1) * P],
                                                    ACT.Exp, bias=neg_max[:, n % 2, c:c + 1],
                                                    accum_out=sums[:, n % 2, c:c + 1])
                    last.then_inc(exp_done, 1)
                g = (n - SPLIT) // GB
                if s == SPLIT % GB and 0 <= g < G:
                    wait(act, kv_affine, 2 * (g + 1), 2 / GB, trip)
                    wait(act, o_ready, GB * (g - 1), 1, trip)
                    nc.scalar.activation(kv_hi[:, g % 2, :, :], kv[:, :, :], ACT.Copy).then_inc(kv_hi_done, 1)
                for what, g, sub, bank, count in uses[n]:
                    sh = shared[bank]
                    if what in ("finish", "residual", "router"):
                        continue
                    wait_shared(act, shared_full, what, g, sub, trip)
                    if what == "turn_kv":
                        wait(act, scores_ready, GB * (g - 1), 1, trip)
                        nc.scalar.activation(kvT_hi[:, g % 2, 2 * sub:2 * sub + 2, :].rearrange("p b j -> p (b j)"),
                                             sh[:, 0:2 * P], ACT.Copy).then_inc(kvT_hi_done, 1)
                    elif what == "query":
                        wait(act, scores_ready, GB * (g - 1), 1, trip)
                        nc.scalar.activation(qT_hi[:, g % 2, :, sub, :], sh[:, :].rearrange("p (b i) -> p b i", b=GB),
                                             ACT.Identity, bias=tb[:, sub:sub + 1]).then_inc(q_hi_done, 1)
                    elif what == "project":
                        wait_shared(act, shared_full, "residual", g - 1, 2, trip)
                        nc.scalar.activation(yT[:, :], sh[:, :], ACT.Identity, bias=tg_bo[:, 0:1],
                                             scale=tg[:, 0:1]).then_inc(shared_out[bank], 1)
                    elif what == "turn_x":
                        wait(act, hid1_ready, E * (g - 1), 1, trip)
                        nc.scalar.activation(xT_hi[:, g % 2, :], sh[:, :], ACT.Copy).then_inc(xT_hi_done, 1)
                    elif what == "turn_cw":
                        wait(act, cw_stored, 16 * g, 16 / GB, trip)
                        wait(act, ffn_done, E * (g - 1) + 1, 1, trip)
                        nc.scalar.activation(cwT[:, :], sh[0:E, :], ACT.Copy).then_inc(shared_out[bank], 1)
                g = n // GB - 1
                if s == 5 and 0 <= g < G:
                    wait(act, router_step, 11 * g + 2, 11 / GB, trip)
                    nc.scalar.activation(prob[:, :, :], shift[:, :, :], ACT.Exp).then_inc(rexp_done, 1)
                f = expert_of(n)
                if f is not None:
                    wait(act, hid1_ready, f + 1, 1, trip)
                    wait(act, hs1_done, f, 1, trip)
                    nc.scalar.activation(hr[:, :], hid[1][:, :], ACT.Relu,
                                         bias=cols[:, 2 * H + 2 * (f % E) + 1:2 * H + 2 * (f % E) + 2]).then_inc(relu_done, 1)
                if 0 <= m < B:
                    wait(act, o_ready, m + 1, 1, trip)
                    if m % GB == 0:
                        wait_shared(act, shared_full, "project", m // GB - 1, 1, trip)
                    b = m % GB
                    nc.scalar.activation(oT[:, :, b * L:(b + 1) * L], o[:, :].rearrange("p (h i) -> p h i", h=H),
                                         ACT.Copy).then_inc(o_out, 1)

            slots(act, slot)

        @block.vector
        def _(dve):
            dve.wait_ge(cols_ready, 1)
            dve.wait_ge(const_step, 8)
            nc.vector.tensor_scalar(neg_b1[:, :], cols[:, 2 * H:2 * H + 2 * E], -1.0, None, ALU.mult).then_inc(diag_ready, 1)
            nc.vector.tensor_copy(b1_diag[:, :, :].rearrange("p e f -> p (e f)")[:, 0:E * E:E + 1],
                                  cols[:, 2 * H:2 * H + 2 * E:2]).then_inc(diag_ready, 1)
            for h in range(H):
                bank = [pT, o][h % 2]
                dve.wait_ge(w_hi, h + 1)
                nc.vector.scalar_tensor_tensor(out=A_lo[:, h, :], in0=bank[:, 0:D], scalar=SCALE,
                                               in1=A_hi[:, h, :].bitcast(F32), op0=ALU.mult, op1=ALU.subtract)
                nc.vector.tensor_copy(M[:, h, :], bank[:, D:2 * D])
                nc.vector.tensor_scalar(tb[:, h:h + 1], bank[:, 2 * D:2 * D + 1], SCALE, None, ALU.mult).then_inc(w_out, 1)
            dve.wait_ge(bias_folded, 1)
            nc.vector.tensor_tensor(bo_sum[:, :], scores[:, 0:1], cols[:, NR - 1:NR], ALU.add).then_inc(bias_ready, 1)
            dve.wait_ge(bias_ready, 1)
            dve.wait_ge(gates_done, 1)
            nc.vector.tensor_tensor(tg_bo[:, :], bo_sum[:, :], tg[:, 0:1], ALU.mult).then_inc(bias_ready, 1)
            dve.wait_ge(bias_folded, 2)
            nc.vector.tensor_tensor(B2[:, :], shared[1][0:E, 0:D], b2_f[:, :], ALU.add).then_inc(bias_ready, 2)
            dve.wait_ge(ffn_hi, 2)
            nc.vector.tensor_tensor(W1_lo[:, :, :, :].rearrange("p e c f -> p (e c) f"), W1_in,
                                    W1_hi[:, :, :, :].rearrange("p e c f -> p (e c) f").bitcast(F32), ALU.subtract)
            nc.vector.tensor_tensor(Wr_lo[:, :], Wr_f[:, :], Wr_hi[:, :].bitcast(F32), ALU.subtract).then_inc(ffn_ready, 1)

            def slot(n, trip):
                s = n % GB
                if 0 <= n < B:
                    wait(dve, scores_ready, n + 1, 1, trip)
                    wait(dve, exp_done, n - 1, 1, trip)
                    nc.vector.tensor_reduce(neg_max[:, n % 2, :], scores[:, :].rearrange("p (c j) -> p c j", c=4),
                                            AX, ALU.max, negate=True).then_inc(max_ready, 1)
                m = n - 1
                if 0 <= m < B:
                    wait(dve, pT_hi_done, m + 1, 1, trip)
                    wait(dve, o_ready, m, 1, trip)
                    nc.vector.tensor_tensor(pT_lo[:, :], pT[:, :], pT_hi[:, :].bitcast(F32),
                                            ALU.subtract).then_inc(pT_lo_done, 1)
                if 0 <= n < B:
                    wait(dve, exp_done, n + 1, 1, trip)
                    wait(dve, probs_ready, n - 1, 1, trip)
                    nc.vector.reciprocal(rsums[:, n % 2, :], sums[:, n % 2, :]).then_inc(rsum_ready, 1)
                g = (n - SPLIT) // GB
                if s == SPLIT % GB and 0 <= g < G:
                    wait(dve, kv_hi_done, g + 1, 1 / GB, trip)
                    wait(dve, o_ready, GB * (g - 1), 1, trip)
                    nc.vector.tensor_tensor(kv_lo[:, g % 2, :, :], kv[:, :, :], kv_hi[:, g % 2, :, :].bitcast(F32),
                                            ALU.subtract).then_inc(kv_lo_done, 1)
                for what, g, sub, bank, count in uses[n]:
                    sh = shared[bank]
                    if what in ("project", "turn_cw"):
                        continue
                    if what == "turn_kv":
                        wait(dve, kvT_hi_done, 4 * g + sub + 1, 4 / GB, trip)
                        wait(dve, scores_ready, GB * (g - 1), 1, trip)
                        nc.vector.tensor_tensor(kvT_lo[:, g % 2, 2 * sub:2 * sub + 2, :].rearrange("p b j -> p (b j)"),
                                                sh[:, 0:2 * P],
                                                kvT_hi[:, g % 2, 2 * sub:2 * sub + 2, :].rearrange("p b j -> p (b j)").bitcast(F32),
                                                ALU.subtract).then_inc(shared_out[bank], 1)
                    elif what == "query":
                        wait(dve, q_hi_done, H * g + sub + 1, 1, trip)
                        wait(dve, scores_ready, GB * (g - 1), 1, trip)
                        nc.vector.scalar_tensor_tensor(out=qT_lo[:, g % 2, :, sub, :],
                                                       in0=sh[:, :].rearrange("p (b i) -> p b i", b=GB),
                                                       scalar=tb[:, sub:sub + 1],
                                                       in1=qT_hi[:, g % 2, :, sub, :].bitcast(F32),
                                                       op0=ALU.add, op1=ALU.subtract).then_inc(shared_out[bank], 1)
                    elif what == "turn_x":
                        wait(dve, xT_hi_done, g + 1, 1 / GB, trip)
                        wait(dve, hid1_ready, E * (g - 1), 1, trip)
                        nc.vector.tensor_tensor(xT_lo[:, g % 2, :], sh[:, :], xT_hi[:, g % 2, :].bitcast(F32),
                                                ALU.subtract).then_inc(shared_out[bank], 1)
                    elif what == "residual":
                        wait_shared(dve, shared_full, what, g, sub, trip)
                        wait(dve, got_xres, 16 * (g + 1), 16 / GB, trip)
                        nc.vector.tensor_tensor(x1[:, g % 2, :, :], sh[:, :].rearrange("p (c d) -> p c d", c=4),
                                                xres[:, :, :], ALU.add).then_inc(shared_out[bank], 1)
                    elif what == "finish":
                        wait_shared(dve, shared_full, what, g, sub, trip)
                        wait(dve, stored, 16 * g, 16 / GB, trip)
                        nc.vector.scalar_tensor_tensor(out=res[:, :, :], in0=sh[:, :].rearrange("p (c d) -> p c d", c=4),
                                                       scalar=tg[:, 1:2], in1=x1[:, g % 2, :, :],
                                                       op0=ALU.mult, op1=ALU.add).then_inc(shared_out[bank], 1)
                    elif what == "router":
                        wait_shared(dve, shared_full, what, g, sub, trip)
                        nc.vector.tensor_tensor(logit[:, :, :], sh[:, 0:4 * E].rearrange("p (c e) -> p c e", c=4),
                                                br_all[:, :].unsqueeze(1).broadcast_to([P, 4, E]),
                                                ALU.add).then_inc(shared_out[bank], 1)
                g = n // GB - 1
                if s == 5 and 0 <= g < G:
                    wait_shared(dve, shared_out, "router", g, 5, trip)
                    nc.vector.tensor_reduce(top[:, :], logit[:, :, :], AX, ALU.max).then_inc(router_step, 1)
                    wait(dve, router_step, 11 * g + 1, 11 / GB, trip)
                    nc.vector.tensor_tensor(shift[:, :, :], logit[:, :, :], top[:, :].unsqueeze(2).broadcast_to([P, 4, E]),
                                            ALU.subtract).then_inc(router_step, 1)
                if s == 3 and 0 <= g < G:
                    wait_shared(dve, shared_out, "residual", g, 2, trip)
                    for c in range(4):
                        last = nc.vector.bn_stats(stats1[:, c, :], x1[:, g % 2, c, :])
                    last.then_inc(stats1_done, 1)
                    count_in_register(dve, g + 1, 1 / GB, trip)
                    dve.wait_ge(const_step, 8)
                    wait(dve, stats1_done, g + 1, 1 / GB, trip)
                    for c in range(4):
                        last = nc.vector.bn_aggr(mv1[:, c, :], stats1[:, c, :])
                    last.then_inc(mv1_done, 1)
                g = (n - STATS) // GB
                if s == STATS % GB and 0 <= g < G:
                    wait(dve, got_kv, 32 * (g + 1), 32 / GB, trip)
                    for b in range(GB):
                        last = nc.vector.bn_stats(stats[:, b, :], kv[:, b, :])
                    last.then_inc(stats_done, 1)
                    wait(dve, rstd_step, 7 * g, 7 / GB, trip)
                    count_in_register(dve, g + 1, 1 / GB, trip)
                    dve.wait_ge(const_step, 8)
                    wait(dve, stats_done, g + 1, 1 / GB, trip)
                    for b in range(GB):
                        last = nc.vector.bn_aggr(mv[:, b, :], stats[:, b, :])
                    last.then_inc(mv_done, 1)
                g = (n - CENTER) // GB
                if s == CENTER % GB and 0 <= g < G:
                    wait(dve, rstd_step, 7 * (g + 1), 7 / GB, trip)
                    for b in range(GB):
                        last = nc.vector.tensor_scalar(kv[:, b, :], kv[:, b, :], mv[:, b, 0:1], rstd[:, b:b + 1],
                                                       ALU.subtract, ALU.mult)
                    last.then_inc(kv_centered, 1)
                f = expert_of(n)
                if f is not None:
                    wait(dve, hid0_ready, f + 1, 1, trip)
                    wait(dve, got_cw[f % 2], 16 * (f // 2 + 1), 8, trip)
                    wait(dve, ffn_done, f - 1, 1, trip)
                    nc.vector.scalar_tensor_tensor(out=hs[:, f % 2, 0, :], in0=hid[0][:, :],
                                                   scalar=neg_b1[:, 2 * (f % E):2 * (f % E) + 1],
                                                   in1=cw_all[:, f % 2, :], op0=ALU.max, op1=ALU.mult).then_inc(hs0_done, 1)
                g = n // GB - 1
                if s == 3 and 0 <= g < G:
                    wait(dve, rstd1_step, 2 * (g + 1), 2 / GB, trip)
                    wait_shared(dve, shared_full, "turn_x", g - 1, 4, trip)
                    for c in range(4):
                        last = nc.vector.tensor_scalar(xn[:, c, :], x1[:, g % 2, c, :], mv1[:, c, 0:1], rstd1[:, c:c + 1],
                                                       ALU.subtract, ALU.mult)
                    last.then_inc(xn_done, 1)
                if s == 5 and 0 <= g < G:
                    at = 11 * g
                    wait(dve, rexp_done, g + 1, 1 / GB, trip)
                    nc.vector.tensor_reduce(psumr[:, :], prob[:, :, :], AX, ALU.add).then_inc(router_step, 1)
                    wait(dve, router_step, at + 3, 11 / GB, trip)
                    nc.vector.reciprocal(prec[:, :], psumr[:, :]).then_inc(router_step, 1)
                    wait(dve, router_step, at + 4, 11 / GB, trip)
                    nc.vector.tensor_tensor(probn[:, :, :], prob[:, :, :], prec[:, :].unsqueeze(2).broadcast_to([P, 4, E]),
                                            ALU.mult).then_inc(router_step, 1)
                    wait(dve, router_step, at + 5, 11 / GB, trip)
                    of_f = probn[:, :, :].unsqueeze(2).broadcast_to([P, 4, E, E])
                    of_e = probn[:, :, :].unsqueeze(3).broadcast_to([P, 4, E, E])
                    nc.vector.tensor_tensor(gt[:, :, :, :], of_f, of_e, ALU.is_gt).then_inc(router_step, 1)
                    nc.vector.tensor_tensor(eq[:, :, :, :], of_f, of_e, ALU.is_equal).then_inc(router_step, 1)
                    wait(dve, router_step, at + 7, 11 / GB, trip)
                    nc.vector.tensor_tensor(eqb[:, :, :, :], eq[:, :, :, :], before[:, :, :].unsqueeze(1).broadcast_to([P, 4, E, E]),
                                            ALU.mult).then_inc(router_step, 1)
                    wait(dve, router_step, at + 8, 11 / GB, trip)
                    nc.vector.tensor_tensor(eq[:, :, :, :], gt[:, :, :, :], eqb[:, :, :, :], ALU.add).then_inc(router_step, 1)
                    wait(dve, router_step, at + 9, 11 / GB, trip)
                    nc.vector.tensor_reduce(rank[:, :, :], eq[:, :, :, :], AX, ALU.add).then_inc(router_step, 1)
                    wait(dve, router_step, at + 10, 11 / GB, trip)
                    wait_shared(dve, shared_full, "turn_cw", g - 1, 6, trip)
                    nc.vector.scalar_tensor_tensor(out=cw[:, :, :], in0=rank[:, :, :], scalar=2.0, in1=probn[:, :, :],
                                                   op0=ALU.is_lt, op1=ALU.mult).then_inc(router_step, 1)

            slots(dve, slot)

        @block.tensor
        def _(pe):
            def three_passes(bank, w_hi_, w_lo_, m_hi, m_lo, start=True, stop=True):
                nc.tensor.matmul(bank, w_hi_, m_hi, start=start, stop=False)
                nc.tensor.matmul(bank, w_hi_, m_lo, start=False, stop=False)
                return nc.tensor.matmul(bank, w_lo_, m_hi, start=False, stop=stop)

            pe.wait_ge(got_rows, 16 * 4)
            pe.wait_ge(const_step, 8)
            nc.tensor.transpose(shared[0][:, 0:NR], rows[:, :], ident[0:NR, 0:NR]).then_inc(cols_turned, 1)
            pe.wait_ge(got_attn_w, 16 * 3)
            pe.wait_ge(cols_ready, 1)
            for h in range(H):
                one, two = hid[h % 2], [pT, o][h % 2]
                if h >= 2:
                    pe.wait_ge(w_out, h - 1)
                for k, w in enumerate((Wq_in[:, h * D:(h + 1) * D], Wkv_in[:, h * D:(h + 1) * D],
                                       Wkv_in[:, (H + h) * D:(H + h + 1) * D])):
                    last = nc.tensor.transpose(one[:, k * P:(k + 1) * P], w, ident[:, :])
                last.then_inc(w_turned, 1)
                pe.wait_ge(w_copied, h + 1)
                WqT, WkT, WvT = (wT[:, h % 2, k * P:(k + 1) * P] for k in range(3))
                nc.tensor.matmul(two[:, 0:D], WqT, WkT, start=True, stop=True)
                nc.tensor.matmul(two[:, D:2 * D], WvT, Wo_in[:, h, :], start=True, stop=True)
                nc.tensor.matmul(two[:, 2 * D:2 * D + 1], WkT, cols[:, h:h + 1], start=True, stop=True).then_inc(w_folded, 1)
            for h in range(H):
                last = nc.tensor.matmul(scores[:, 0:1], Wo_in[:, h, :], cols[:, H + h:H + h + 1],
                                        start=(h == 0), stop=(h == H - 1))
            last.then_inc(bias_folded, 1)
            pe.wait_ge(diag_ready, 2)
            pe.wait_ge(got_ffn_w, 16 * 3)
            for e in range(E):
                last = nc.tensor.matmul(shared[1][0:E, 0:D], b1_diag[:, e, :], W2_sb[:, e, 0, :],
                                        start=(e == 0), stop=(e == E - 1))
            last.then_inc(bias_folded, 1)
            pe.wait_ge(bias_ready, 4)
            pe.wait_ge(ffn_ready, 1)

            def slot(n, trip):
                if 0 <= n < B:
                    g, b = n // GB, n % GB
                    if b == 0:
                        wait_shared(pe, shared_out, "query", g, 6, trip)
                        wait_shared(pe, shared_out, "query", g, 7, trip)
                    wait(pe, exp_done, n, 1, trip)
                    for c in range(4):
                        q_hi, q_lo = (q[:, g % 2, b, 2 * c:2 * c + 2, :].rearrange("p h i -> p (h i)")
                                      for q in (qT_hi, qT_lo))
                        last = three_passes(scores[:, c * P:(c + 1) * P], q_hi, q_lo,
                                            kvT_hi[:, g % 2, b, :], kvT_lo[:, g % 2, b, :])
                    last.then_inc(scores_ready, 1)
                m = n - 1
                if 0 <= m < B:
                    wait(pe, probs_ready, m + 1, 1, trip)
                    wait(pe, pT_lo_done, m, 1, trip)
                    for c in range(4):
                        last = nc.tensor.transpose(pT[:, c * P:(c + 1) * P], probs[:, m % 2, c * P:(c + 1) * P], ident[:, :])
                    last.then_inc(pT_ready, 1)
                f = expert_of(n - 1)
                if f is not None:
                    g, e = f // E, f % E
                    if e == 0:
                        wait(pe, f_done, g, 1 / GB, trip)
                        wait_shared(pe, shared_out, "turn_cw", g, 6, trip)
                        nc.tensor.matmul(acc[:, :], B2[:, :], cwT[:, :], start=True, stop=False)
                    wait(pe, hs0_done, f + 1, 1, trip)
                    nc.tensor.matmul(acc[:, :], W2_sb[:, e, 0, :], hs[:, f % 2, 0, :], start=False, stop=False)
                    wait(pe, hs1_done, f + 1, 1, trip)
                    nc.tensor.matmul(acc[:, :], W2_sb[:, e, 1, :], hs[:, f % 2, 1, :], start=False,
                                     stop=(e == E - 1)).then_inc(ffn_done, 1)
                for what, g, sub, bank, count in uses[n]:
                    sh = shared[bank]
                    if count > 0:
                        pe.wait_ge(shared_out[bank], count + trip * shared_per_trip)
                    if what == "turn_kv":
                        wait(pe, kv_affine, 2 * (g + 1), 2 / GB, trip)
                        for i in range(2):
                            last = nc.tensor.transpose(sh[:, i * P:(i + 1) * P], kv[:, 2 * sub + i, :], ident[:, :])
                    elif what == "query":
                        if sub == 0:
                            wait_shared(pe, shared_out, "turn_kv", g, 1, trip)
                            wait_shared(pe, shared_out, "turn_kv", g, 3, trip)
                        last = three_passes(sh[:, :].rearrange("p (b i) -> p b i", b=GB), A_hi[:, sub, :], A_lo[:, sub, :],
                                            kvT_hi[:, g % 2, :, L:P], kvT_lo[:, g % 2, :, L:P])
                    elif what == "project":
                        wait(pe, o_out, GB * (g + 1), 1, trip)
                        for h in range(H):
                            last = nc.tensor.matmul(sh[:, :], M[:, h, :], oT[:, h, :], start=(h == 0), stop=(h == H - 1))
                    elif what == "residual":
                        wait_shared(pe, shared_out, "project", g, 1, trip)
                        for c in range(4):
                            last = nc.tensor.transpose(sh[:, c * P:(c + 1) * P], yT[:, c * P:(c + 1) * P], ident[:, :])
                    elif what == "turn_x":
                        wait(pe, xn_done, g + 1, 1 / GB, trip)
                        for c in range(4):
                            last = nc.tensor.transpose(sh[:, c * P:(c + 1) * P], xn[:, c, :], ident[:, :])
                    elif what == "router":
                        wait_shared(pe, shared_out, "turn_x", g, 4, trip)
                        for c in range(4):
                            rows_c = slice(c * P, (c + 1) * P)
                            last = three_passes(sh[:, c * E:(c + 1) * E], xT_hi[:, g % 2, rows_c], xT_lo[:, g % 2, rows_c],
                                                Wr_hi[:, :], Wr_lo[:, :])
                    elif what == "turn_cw":
                        wait(pe, router_step, 11 * (g + 1), 11 / GB, trip)
                        for c in range(4):
                            last = nc.tensor.transpose(sh[0:E, c * P:(c + 1) * P], cw[:, c, :], ident[:, :])
                    elif what == "finish":
                        wait(pe, f_done, g + 1, 1 / GB, trip)
                        for c in range(4):
                            last = nc.tensor.transpose(sh[:, c * P:(c + 1) * P], fT[:, c * P:(c + 1) * P], ident[:, :])
                    last.then_inc(shared_full[bank], 1)
                f = expert_of(n)
                if f is not None:
                    g, e = f // E, f % E
                    if e == 0:
                        wait_shared(pe, shared_out, "turn_x", g, 4, trip)
                    for c, (done, ready) in enumerate(((hs0_done, hid0_ready), (relu_done, hid1_ready))):
                        wait(pe, done, f, 1, trip)
                        three_passes(hid[c][:, :], W1_hi[:, e, c, :], W1_lo[:, e, c, :],
                                     xT_hi[:, g % 2, :], xT_lo[:, g % 2, :]).then_inc(ready, 1)
                if 0 <= m < B:
                    wait(pe, pT_lo_done, m + 1, 1, trip)
                    wait(pe, kv_lo_done, m // GB + 1, 1 / GB, trip)
                    wait(pe, o_out, m, 1, trip)
                    g, b = m // GB, m % GB
                    three_passes(o[:, :], kv_hi[:, g % 2, b, :], kv_lo[:, g % 2, b, :],
                                 pT_hi[:, :], pT_lo[:, :]).then_inc(o_ready, 1)

            slots(pe, slot)


_INS = ['x', 'ctx_1024', 'g_xattn', 'g_ffn', 'L0_xattn_gamma_media', 'L0_xattn_beta_media', 'L0_xattn_gamma_lat',
        'L0_xattn_beta_lat', 'L0_xattn_Wq', 'L0_xattn_bq', 'L0_xattn_Wkv', 'L0_xattn_bkv', 'L0_xattn_Wo',
        'L0_xattn_bo', 'L0_ffn_Wr', 'L0_ffn_br', 'L0_ffn_W1', 'L0_ffn_b1', 'L0_ffn_W2', 'L0_ffn_b2']
_OUTS = [((B, L, D), 'float32')]


def kernel(**inputs):
    import numpy as _np
    import concourse.bacc as _bacc
    from concourse import mybir as _mybir
    from concourse.bass_utils import run_bass_kernel_spmd as _run

    nc = _bacc.Bacc("TRN2", target_bir_lowering=False, num_devices=1)
    arrays, args = {}, []
    for name in _INS:
        a = _np.ascontiguousarray(inputs[name])
        arrays[f"in_{name}_dram"] = a
        args.append(nc.dram_tensor(f"in_{name}_dram", a.shape, _mybir.dt.from_np(a.dtype), kind="ExternalInput").ap())
    for i, (shape, dtype) in enumerate(_OUTS):
        dt = _mybir.dt.from_np(_np.dtype(dtype))
        args.append(nc.dram_tensor(f"out_{i}_dram", shape, dt, kind="ExternalOutput").ap())
    flamingo(nc, *args)
    r = _run(nc, [arrays], core_ids=[0])
    got = tuple(r.results[0][f"out_{i}_dram"] for i in range(len(_OUTS)))
    return got[0]
```

```python
from contextlib import ExitStack

import concourse.bass as bass
from concourse import mybir

F32 = mybir.dt.float32
F32R = mybir.dt.float32r
ALU = mybir.AluOpType
ACT = mybir.ActivationFunctionType
AX = mybir.AxisListType.X

P = 128
D = 128
B = 128
L = 64
H = 8
E = 8
GB = 8
G = B // GB
TOK = GB * L
EPS = 1e-5
SCALE = float(D) ** -0.5

LOAD, STATS, CENTER = -12, -11, -10
AFFINE = (-9, -9, -8, -7)
SPLIT = -6
FFN = 15
FIRST, LAST = LOAD, GB * (G - 1) + 26
PER_TRIP = 2 * GB
LOOP_AT, TRIPS = 32, 5

SHARED = {
    0: [("turn_kv", 1)],
    1: [("turn_kv", 1), ("project", -1)],
    2: [("turn_kv", 1), ("finish", -3), ("residual", -1)],
    3: [("turn_kv", 1)],
    4: [("query", 1), ("turn_x", -1), ("query", 1)],
    5: [("query", 1), ("router", -1), ("query", 1)],
    6: [("query", 1), ("turn_cw", -1), ("query", 1)],
    7: [("query", 1), ("query", 1)],
}


def plan_shared():
    uses, used = {}, [0, 0]
    for n in range(FIRST, LAST + 1):
        g, s = n // GB, n % GB
        at = sum(len(SHARED[t]) for t in range(s))
        uses[n] = []
        heads = 0
        for what, off in SHARED[s]:
            bank, at = at % 2, at + 1
            sub = 2 * (s - 4) + heads if what == "query" else s
            heads += what == "query"
            if 0 <= g + off < G:
                uses[n].append((what, g + off, sub, bank, used[bank]))
                used[bank] += 1
    return uses


def flamingo(nc, x, ctx_in, g_xattn, g_ffn, gamma_m, beta_m, gamma_l, beta_l, Wq, bq, Wkv, bkv, Wo, bo,
             Wr, br, W1, b1, W2, b2, out):
    uses = plan_shared()
    use_at = {(what, g, sub): (bank, before) for n in uses for what, g, sub, bank, before in uses[n]}
    shared_per_trip = sum(len(v) for v in SHARED.values())

    ctx = ExitStack()
    with ctx:
        def sb(name, shape, dt=F32):
            return ctx.enter_context(nc.sbuf_tensor(name, shape, dt))

        def psum(name):
            return ctx.enter_context(nc.psum_tensor(name, [P, 512], F32))

        def sem(name):
            return ctx.enter_context(nc.semaphore(name))

        kv = sb("kv", [P, GB, D])
        kv_hi = sb("kv_hi", [P, 2, GB, D], F32R)
        kv_lo = sb("kv_lo", [P, 2, GB, D], F32R)
        kvT = sb("kvT", [P, 2, GB, P])
        latT_hi = sb("latT_hi", [P, GB, L], F32R)
        latT_lo = sb("latT_lo", [P, GB, L], F32R)
        qT = sb("qT", [P, 2, GB, H, L])
        probs = sb("probs", [P, 2, 512])
        pT_hi = sb("pT_hi", [P, 512], F32R)
        pT_lo = sb("pT_lo", [P, 512], F32R)
        oT = sb("oT", [P, H, TOK])
        yT = sb("yT", [P, TOK])
        xres = sb("xres", [P, 4, D])
        x1 = sb("x1", [P, 2, 4, D])
        xn = sb("xn", [P, 4, D])
        xT_hi = sb("xT_hi", [P, 2, TOK], F32R)
        xT_lo = sb("xT_lo", [P, 2, TOK], F32R)
        cwT = sb("cwT", [E, TOK])
        cw_all = sb("cw_all", [P, 2, TOK])
        hs = sb("hs", [P, 2, 2, TOK])
        hr = sb("hr", [P, TOK])
        fT = sb("fT", [P, TOK])
        res = sb("res", [P, 4, D])
        A_hi = sb("A_hi", [P, H, D], F32R)
        A_lo = sb("A_lo", [P, H, D], F32R)
        M = sb("M", [P, H, D])
        W1_hi = sb("W1_hi", [P, E, 2, P], F32R)
        W1_lo = sb("W1_lo", [P, E, 2, P], F32R)
        W2_sb = sb("W2_sb", [P, E, 2, D])
        Wr_f = sb("Wr_f", [P, E])
        Wr_hi = sb("Wr_hi", [P, E], F32R)
        Wr_lo = sb("Wr_lo", [P, E], F32R)
        NR = 2 * H + 2 * E + 1
        rows = sb("rows", [NR, D])
        cols = sb("cols", [P, NR])
        tb = sb("tb", [P, H])
        neg_b1 = sb("neg_b1", [P, 2 * E])
        b1_diag = sb("b1_diag", [P, E, E])
        b2_f = sb("b2_f", [E, D])
        B2 = sb("B2", [E, D])
        gamma = sb("gamma", [P, D])
        beta = sb("beta", [P, D])
        br_all = sb("br_all", [P, E])
        gates = sb("gates", [P, 2])
        tg = sb("tg", [P, 2])
        bo_sum = sb("bo_sum", [P, 1])
        tg_bo = sb("tg_bo", [P, 1])
        ident = sb("ident", [P, P])
        ones_sq = sb("ones_sq", [P, P])
        before = sb("before", [P, E, E])
        neg_half = sb("neg_half", [P, GB])
        ones_col = sb("ones_col", [P, 2])
        var_mul = sb("var_mul", [P, 1])
        var_add = sb("var_add", [P, 1])
        stats = sb("stats", [P, GB, 6])
        mv = sb("mv", [P, GB, 2])
        rstd = sb("rstd", [P, GB])
        var_eps = sb("var_eps", [P, GB])
        neg_max = sb("neg_max", [P, 2, 4])
        sums = sb("sums", [P, 2, 4])
        rsums = sb("rsums", [P, 2, 4])
        stats1 = sb("stats1", [P, 4, 6])
        mv1 = sb("mv1", [P, 4, 2])
        var_eps1 = sb("var_eps1", [P, 4])
        rstd1 = sb("rstd1", [P, 4])
        logit = sb("logit", [P, 4, E])
        shift = sb("shift", [P, 4, E])
        prob = sb("prob", [P, 4, E])
        probn = sb("probn", [P, 4, E])
        top = sb("top", [P, 4])
        psumr = sb("psumr", [P, 4])
        prec = sb("prec", [P, 4])
        gt = sb("gt", [P, 4, E, E])
        eq = sb("eq", [P, 4, E, E])
        eqb = sb("eqb", [P, 4, E, E])
        rank = sb("rank", [P, 4, E])
        cw = sb("cw", [P, 4, E])
        Wq_in = oT[:, 0:2, :].rearrange("p a n -> p (a n)")
        Wkv_in = oT[:, 2:6, :].rearrange("p a n -> p (a n)")
        Wo_in = oT[:, 6:8, :].rearrange("p a n -> p (a n)").rearrange("p (h n) -> p h n", h=H)
        W1_in = hs[:, :, :, :].rearrange("p a c (k f) -> p (a c k) f", f=P)
        wT = probs

        scores = psum("scores")
        pT = psum("pT")
        o = psum("o")
        hid = [psum("hid0"), psum("hid1")]
        acc = psum("acc")
        shared = [psum("shared0"), psum("shared1")]

        cw_dram = nc.dram_tensor("cw_rows", (2, E, TOK), F32).ap()

        got_rows = sem("got_rows")
        got_attn_w = sem("got_attn_w")
        got_ffn_w = sem("got_ffn_w")
        got_small = sem("got_small")
        got_kv = sem("got_kv")
        got_xres = sem("got_xres")
        const_step = sem("const_step")
        gates_done = sem("gates_done")
        cols_turned = sem("cols_turned")
        cols_ready = sem("cols_ready")
        w_turned = sem("w_turned")
        w_copied = sem("w_copied")
        w_folded = sem("w_folded")
        w_hi = sem("w_hi")
        w_out = sem("w_out")
        bias_folded = sem("bias_folded")
        bias_ready = sem("bias_ready")
        diag_ready = sem("diag_ready")
        ffn_hi = sem("ffn_hi")
        ffn_ready = sem("ffn_ready")
        stats_done = sem("stats_done")
        mv_done = sem("mv_done")
        rstd_done = sem("rstd_done")
        kv_centered = sem("kv_centered")
        kv_affine = sem("kv_affine")
        kv_hi_done = sem("kv_hi_done")
        kv_lo_done = sem("kv_lo_done")
        scores_ready = sem("scores_ready")
        max_ready = sem("max_ready")
        exp_done = sem("exp_done")
        rsum_ready = sem("rsum_ready")
        probs_ready = sem("probs_ready")
        pT_ready = sem("pT_ready")
        pT_hi_done = sem("pT_hi_done")
        pT_lo_done = sem("pT_lo_done")
        o_ready = sem("o_ready")
        o_out = sem("o_out")
        stats1_done = sem("stats1_done")
        mv1_done = sem("mv1_done")
        rstd1_done = sem("rstd1_done")
        xn_done = sem("xn_done")
        router_step = sem("router_step")
        rexp_done = sem("rexp_done")
        cw_stored = sem("cw_stored")
        got_cw = [sem("got_cw_even"), sem("got_cw_odd")]
        hid0_ready = sem("hid0_ready")
        hid1_ready = sem("hid1_ready")
        hs0_done = sem("hs0_done")
        relu_done = sem("relu_done")
        hs1_done = sem("hs1_done")
        ffn_done = sem("ffn_done")
        f_done = sem("f_done")
        stored = sem("stored")
        shared_full = [sem("shared_full0"), sem("shared_full1")]
        shared_out = [sem("shared_out0"), sem("shared_out1")]
        latT_done = sem("latT_done")
        xT_hi_done = sem("xT_hi_done")

        def slots(eng, body):
            for n in range(FIRST, LOOP_AT):
                body(n, 0)
            with eng.Fori(0, TRIPS) as trip:
                for n in range(LOOP_AT, LOOP_AT + PER_TRIP):
                    body(n, trip)
            for n in range(LOOP_AT + PER_TRIP * TRIPS, LAST + 1):
                body(n, 0)

        def wait(eng, s, value, per_slot, trip):
            if value > 0:
                eng.wait_ge(s, value + trip * int(per_slot * PER_TRIP))

        def wait_shared(eng, sems, what, g, sub, trip):
            if (what, g, sub) in use_at:
                bank, count = use_at[what, g, sub]
                eng.wait_ge(sems[bank], count + 1 + trip * shared_per_trip)

        def count_in_register(eng, value, per_slot, trip):
            if not isinstance(trip, int):
                eng.compute_val(value + trip * int(per_slot * PER_TRIP))

        def first_row(eng, g, trip):
            return g * GB if isinstance(trip, int) else eng.snap((g + 2 * trip) * GB)

        def expert_of(n):
            f = n - FFN
            return f if 0 <= f < G * E else None

        block = ctx.enter_context(nc.Block())

        @block.sync
        def _(sp):
            sp.dma_start(rows[0:H, :], bq.rearrange("(h d) -> h d", h=H)).then_inc(got_rows, 16)
            sp.dma_start(rows[H:2 * H, :], bkv[H * D:2 * H * D].rearrange("(h d) -> h d", h=H)).then_inc(got_rows, 16)
            sp.dma_start(rows[2 * H:2 * H + 2 * E, :], b1.rearrange("e (c f) -> (e c) f", c=2)).then_inc(got_rows, 16)
            sp.dma_start(rows[NR - 1:NR, :], bo.rearrange("(a n) -> a n", a=1)).then_inc(got_rows, 16)
            sp.dma_start(Wq_in, Wq).then_inc(got_attn_w, 16)
            sp.dma_start(Wkv_in, Wkv).then_inc(got_attn_w, 16)
            sp.dma_start(Wo_in, Wo.rearrange("(h e) n -> e h n", h=H)).then_inc(got_attn_w, 16)

            def slot(n, trip):
                s = n % GB
                g = (n - LOAD) // GB
                if s == LOAD % GB and 0 <= g < G:
                    at = bass.ds(first_row(sp, g, trip), GB)
                    count_in_register(sp, 2 * g, 2 / GB, trip)
                    count_in_register(sp, g, 1 / GB, trip)
                    wait(sp, latT_done, 2 * g, 2 / GB, trip)
                    wait(sp, kv_hi_done, g, 1 / GB, trip)
                    wait(sp, kv_lo_done, g, 1 / GB, trip)
                    sp.dma_start(kv[0:L, :, :], ctx_in[at, :, :].rearrange("b s d -> s b d")).then_inc(got_kv, 16)
                    sp.dma_start(kv[L:P, :, :], x[at, :, :].rearrange("b s d -> s b d")).then_inc(got_kv, 16)
                g = n // GB
                if s == 4 and 0 <= g < G:
                    at = bass.ds(first_row(sp, g, trip), GB)
                    wait_shared(sp, shared_out, "residual", g - 1, 2, trip)
                    sp.dma_start(xres[:, :, :], x[at, :, :].rearrange("(c b) s d -> (b s) c d", b=2)).then_inc(got_xres, 16)
                g = n // GB - 1
                if s == 6 and 0 <= g < G:
                    count_in_register(sp, 8 * E * (g - 1), 8, trip)
                    wait_shared(sp, shared_out, "turn_cw", g, 6, trip)
                    wait(sp, got_cw[0], 8 * E * (g - 1), 8, trip)
                    wait(sp, got_cw[1], 8 * E * (g - 1), 8, trip)
                    sp.dma_start(cw_dram[g % 2, :, :], cwT[:, :]).then_inc(cw_stored, 16)
                f = expert_of(n + 1)
                if f is not None:
                    stored_count, used_count = 16 * (f // E + 1) + trip * 32, f - 1 + trip * PER_TRIP
                    count_in_register(sp, 16 * (f // E + 1), 16 / GB, trip)
                    count_in_register(sp, f - 1, 1, trip)
                    sp.wait_ge(cw_stored, stored_count)
                    if f > 1:
                        sp.wait_ge(hs0_done, used_count)
                        sp.wait_ge(hs1_done, used_count)
                    sp.dma_start(cw_all[:, f % 2, :],
                                 cw_dram[f // E % 2, f % E, :].partition_broadcast(P)).then_inc(got_cw[f % 2], 16)
                g = n // GB - 3
                if s == 2 and 0 <= g < G:
                    at = bass.ds(first_row(sp, g, trip), GB)
                    wait_shared(sp, shared_out, "finish", g, 2, trip)
                    sp.dma_start(out[at, :, :].rearrange("(c b) s d -> (b s) c d", b=2), res[:, :, :]).then_inc(stored, 16)

            slots(sp, slot)
            sp.wait_ge(stored, 16 * G)
            sp.wait_ge(cw_stored, 16 * G)

        @block.gpsimd
        def _(pool):
            nc.gpsimd.memset(neg_half[:, :], -0.5).then_inc(const_step, 1)
            nc.gpsimd.memset(ones_col[:, 0:1], 1.0 + EPS).then_inc(const_step, 1)
            nc.gpsimd.memset(ones_col[:, 1:2], EPS * EPS).then_inc(const_step, 1)
            nc.gpsimd.memset(ones_sq[:, :], 1.0).then_inc(const_step, 1)
            nc.gpsimd.memset(b1_diag[:, :, :], 0.0).then_inc(const_step, 1)
            nc.gpsimd.memset(eq[:, 0, :, :], 1.0).then_inc(const_step, 1)
            pool.wait_ge(const_step, 6)
            nc.gpsimd.affine_select(out=var_mul[:, :], in_=ones_col[:, 0:1], compare_op=ALU.is_ge, fill=1.0,
                                    base=-L, pattern=[[0, 1]], channel_multiplier=1).then_inc(const_step, 1)
            nc.gpsimd.affine_select(out=var_add[:, :], in_=ones_col[:, 1:2], compare_op=ALU.is_ge, fill=EPS,
                                    base=-L, pattern=[[0, 1]], channel_multiplier=1).then_inc(const_step, 1)
            nc.gpsimd.affine_select(out=ident[:, :], in_=ones_sq[:, :], compare_op=ALU.is_equal, fill=0.0,
                                    base=0, pattern=[[-1, P]], channel_multiplier=1).then_inc(const_step, 1)
            nc.gpsimd.affine_select(out=before[:, :, :], in_=eq[:, 0, :, :], compare_op=ALU.is_gt, fill=0.0,
                                    base=0, pattern=[[1, E], [-1, E]], channel_multiplier=0).then_inc(const_step, 1)
            pool.wait_ge(got_small, 16 * 8)

            def slot(n, trip):
                s = n % GB
                if 0 <= n < B:
                    wait(pool, rsum_ready, n + 1, 1, trip)
                    pv = probs[:, n % 2, :].rearrange("p (c j) -> p c j", c=4)
                    nc.gpsimd.tensor_tensor(pv, pv, rsums[:, n % 2, :].unsqueeze(2).broadcast_to([P, 4, P]),
                                            ALU.mult).then_inc(probs_ready, 1)
                g = (n - STATS) // GB
                if s == STATS % GB and 0 <= g < G:
                    wait(pool, mv_done, 2 * (g + 1), 2 / GB, trip)
                    nc.gpsimd.tensor_tensor(rstd[:, :], var_eps[:, :], neg_half[:, :], ALU.pow).then_inc(rstd_done, 1)
                for k in range(4):
                    g = (n - AFFINE[k]) // GB
                    if s == AFFINE[k] % GB and 0 <= g < G:
                        pair = kv[:, 2 * k:2 * k + 2, :]
                        wait(pool, kv_centered, g + 1, 1 / GB, trip)
                        nc.gpsimd.tensor_tensor(pair, pair, gamma[:, :].unsqueeze(1).broadcast_to([P, 2, D]),
                                                ALU.mult).then_inc(kv_affine, 1)
                        wait(pool, kv_affine, 8 * g + 2 * k + 1, 8 / GB, trip)
                        nc.gpsimd.tensor_tensor(pair, pair, beta[:, :].unsqueeze(1).broadcast_to([P, 2, D]),
                                                ALU.add).then_inc(kv_affine, 1)
                g = n // GB - 1
                if s == 3 and 0 <= g < G:
                    wait(pool, mv1_done, 2 * (g + 1), 2 / GB, trip)
                    nc.gpsimd.tensor_tensor(rstd1[:, :], var_eps1[:, :], neg_half[:, 0:4], ALU.pow).then_inc(rstd1_done, 1)
                f = expert_of(n)
                if f is not None:
                    wait(pool, relu_done, f + 1, 1, trip)
                    wait(pool, got_cw[f % 2], 16 * (f // 2 + 1), 8, trip)
                    wait(pool, ffn_done, f - 1, 1, trip)
                    nc.gpsimd.tensor_tensor(hs[:, f % 2, 1, :], hr[:, :], cw_all[:, f % 2, :],
                                            ALU.mult).then_inc(hs1_done, 1)

            slots(pool, slot)

        @block.scalar
        def _(act):
            act.dma_start(gates[:, 0:1], g_xattn.partition_broadcast(P)).then_inc(got_small, 16)
            act.dma_start(gates[:, 1:2], g_ffn.partition_broadcast(P)).then_inc(got_small, 16)
            act.dma_start(gamma[0:L, :], gamma_m.partition_broadcast(L)).then_inc(got_small, 16)
            act.dma_start(gamma[L:P, :], gamma_l.partition_broadcast(L)).then_inc(got_small, 16)
            act.dma_start(beta[0:L, :], beta_m.partition_broadcast(L)).then_inc(got_small, 16)
            act.dma_start(beta[L:P, :], beta_l.partition_broadcast(L)).then_inc(got_small, 16)
            act.dma_start(br_all[:, :], br.partition_broadcast(P)).then_inc(got_small, 16)
            act.dma_start(b2_f[:, :], b2).then_inc(got_small, 16)
            act.dma_start(W1_in.rearrange("p (e c) f -> p e (c f)", c=2), W1.rearrange("e d f -> d e f")).then_inc(got_ffn_w, 16)
            act.dma_start(W2_sb[:, :, :, :], W2.rearrange("e (c f) n -> f e c n", c=2)).then_inc(got_ffn_w, 16)
            act.dma_start(Wr_f[:, :], Wr).then_inc(got_ffn_w, 16)
            act.wait_ge(got_small, 16 * 8)
            nc.scalar.activation(tg[:, :], gates[:, :], ACT.Tanh).then_inc(gates_done, 1)
            act.wait_ge(cols_turned, 1)
            nc.scalar.activation(cols[:, :], shared[0][:, 0:NR], ACT.Copy).then_inc(cols_ready, 1)
            for h in range(H):
                act.wait_ge(w_turned, h + 1)
                if h >= 2:
                    act.wait_ge(w_folded, h - 1)
                nc.scalar.activation(wT[:, h % 2, 0:3 * P], hid[h % 2][:, 0:3 * P], ACT.Copy).then_inc(w_copied, 1)
                act.wait_ge(w_folded, h + 1)
                nc.scalar.activation(A_hi[:, h, :], [pT, o][h % 2][:, 0:D], ACT.Copy, scale=SCALE).then_inc(w_hi, 1)
            act.wait_ge(got_ffn_w, 16 * 3)
            nc.scalar.activation(W1_hi[:, :, :, :].rearrange("p e c f -> p (e c) f"), W1_in, ACT.Copy).then_inc(ffn_hi, 1)
            nc.scalar.activation(Wr_hi[:, :], Wr_f[:, :], ACT.Copy).then_inc(ffn_hi, 1)
            act.wait_ge(bias_ready, 4)

            def slot(n, trip):
                s = n % GB
                g = n // GB - 3
                if s == 1 and 0 <= g < G:
                    wait(act, ffn_done, E * (g + 1), 1, trip)
                    wait_shared(act, shared_full, "finish", g - 1, 2, trip)
                    nc.scalar.activation(fT[:, :], acc[:, :], ACT.Copy).then_inc(f_done, 1)
                m = n - 1
                if 0 <= m < B:
                    wait(act, pT_ready, m + 1, 1, trip)
                    wait(act, o_ready, m, 1, trip)
                    nc.scalar.activation(pT_hi[:, :], pT[:, :], ACT.Copy).then_inc(pT_hi_done, 1)
                if 0 <= n < B:
                    wait(act, max_ready, n + 1, 1, trip)
                    wait(act, pT_ready, n - 1, 1, trip)
                    wait(act, rsum_ready, n - 1, 1, trip)
                    for c in range(4):
                        last = nc.scalar.activation(probs[:, n % 2, c * P:(c + 1) * P], scores[:, c * P:(c + 1) * P],
                                                    ACT.Exp, bias=neg_max[:, n % 2, c:c + 1],
                                                    accum_out=sums[:, n % 2, c:c + 1])
                    last.then_inc(exp_done, 1)
                g = (n - SPLIT) // GB
                if s == SPLIT % GB and 0 <= g < G:
                    wait(act, kv_affine, 8 * (g + 1), 8 / GB, trip)
                    wait(act, o_ready, GB * (g - 1), 1, trip)
                    nc.scalar.activation(kv_hi[:, g % 2, :, :], kv[:, :, :], ACT.Copy).then_inc(kv_hi_done, 1)
                for what, g, sub, bank, count in uses[n]:
                    sh = shared[bank]
                    if what in ("finish", "residual", "router"):
                        continue
                    wait_shared(act, shared_full, what, g, sub, trip)
                    if what == "turn_kv":
                        wait(act, scores_ready, GB * (g - 1), 1, trip)
                        nc.scalar.activation(kvT[:, g % 2, 2 * sub:2 * sub + 2, :].rearrange("p b j -> p (b j)"),
                                             sh[:, 0:2 * P], ACT.Copy).then_inc(shared_out[bank], 1)
                    elif what == "query":
                        wait(act, scores_ready, GB * (g - 1), 1, trip)
                        nc.scalar.activation(qT[:, g % 2, :, sub, :], sh[:, :].rearrange("p (b i) -> p b i", b=GB),
                                             ACT.Identity, bias=tb[:, sub:sub + 1]).then_inc(shared_out[bank], 1)
                    elif what == "project":
                        wait_shared(act, shared_full, "residual", g - 1, 2, trip)
                        nc.scalar.activation(yT[:, :], sh[:, :], ACT.Identity, bias=tg_bo[:, 0:1],
                                             scale=tg[:, 0:1]).then_inc(shared_out[bank], 1)
                    elif what == "turn_x":
                        wait(act, hid1_ready, E * (g - 1), 1, trip)
                        nc.scalar.activation(xT_hi[:, g % 2, :], sh[:, :], ACT.Copy).then_inc(xT_hi_done, 1)
                    elif what == "turn_cw":
                        wait(act, cw_stored, 16 * g, 16 / GB, trip)
                        wait(act, ffn_done, E * (g - 1) + 1, 1, trip)
                        nc.scalar.activation(cwT[:, :], sh[0:E, :], ACT.Copy).then_inc(shared_out[bank], 1)
                g = n // GB - 1
                if s == 5 and 0 <= g < G:
                    wait(act, router_step, 11 * g + 2, 11 / GB, trip)
                    nc.scalar.activation(prob[:, :, :], shift[:, :, :], ACT.Exp).then_inc(rexp_done, 1)
                f = expert_of(n)
                if f is not None:
                    wait(act, hid1_ready, f + 1, 1, trip)
                    wait(act, hs1_done, f, 1, trip)
                    nc.scalar.activation(hr[:, :], hid[1][:, :], ACT.Relu,
                                         bias=cols[:, 2 * H + 2 * (f % E) + 1:2 * H + 2 * (f % E) + 2]).then_inc(relu_done, 1)
                if 0 <= m < B:
                    wait(act, o_ready, m + 1, 1, trip)
                    if m % GB == 0:
                        wait_shared(act, shared_full, "project", m // GB - 1, 1, trip)
                    b = m % GB
                    nc.scalar.activation(oT[:, :, b * L:(b + 1) * L], o[:, :].rearrange("p (h i) -> p h i", h=H),
                                         ACT.Copy).then_inc(o_out, 1)

            slots(act, slot)

        @block.vector
        def _(dve):
            dve.wait_ge(cols_ready, 1)
            dve.wait_ge(const_step, 10)
            nc.vector.tensor_scalar(neg_b1[:, :], cols[:, 2 * H:2 * H + 2 * E], -1.0, None, ALU.mult).then_inc(diag_ready, 1)
            nc.vector.tensor_copy(b1_diag[:, :, :].rearrange("p e f -> p (e f)")[:, 0:E * E:E + 1],
                                  cols[:, 2 * H:2 * H + 2 * E:2]).then_inc(diag_ready, 1)
            for h in range(H):
                bank = [pT, o][h % 2]
                dve.wait_ge(w_hi, h + 1)
                nc.vector.scalar_tensor_tensor(out=A_lo[:, h, :], in0=bank[:, 0:D], scalar=SCALE,
                                               in1=A_hi[:, h, :].bitcast(F32), op0=ALU.mult, op1=ALU.subtract)
                nc.vector.tensor_copy(M[:, h, :], bank[:, D:2 * D])
                nc.vector.tensor_scalar(tb[:, h:h + 1], bank[:, 2 * D:2 * D + 1], SCALE, None, ALU.mult).then_inc(w_out, 1)
            dve.wait_ge(bias_folded, 1)
            nc.vector.tensor_tensor(bo_sum[:, :], scores[:, 0:1], cols[:, NR - 1:NR], ALU.add).then_inc(bias_ready, 1)
            dve.wait_ge(bias_ready, 1)
            dve.wait_ge(gates_done, 1)
            nc.vector.tensor_tensor(tg_bo[:, :], bo_sum[:, :], tg[:, 0:1], ALU.mult).then_inc(bias_ready, 1)
            dve.wait_ge(bias_folded, 2)
            nc.vector.tensor_tensor(B2[:, :], shared[1][0:E, 0:D], b2_f[:, :], ALU.add).then_inc(bias_ready, 2)
            dve.wait_ge(ffn_hi, 2)
            nc.vector.tensor_tensor(W1_lo[:, :, :, :].rearrange("p e c f -> p (e c) f"), W1_in,
                                    W1_hi[:, :, :, :].rearrange("p e c f -> p (e c) f").bitcast(F32), ALU.subtract)
            nc.vector.tensor_tensor(Wr_lo[:, :], Wr_f[:, :], Wr_hi[:, :].bitcast(F32), ALU.subtract).then_inc(ffn_ready, 1)

            def slot(n, trip):
                s = n % GB
                if 0 <= n < B:
                    wait(dve, scores_ready, n + 1, 1, trip)
                    wait(dve, exp_done, n - 1, 1, trip)
                    nc.vector.tensor_reduce(neg_max[:, n % 2, :], scores[:, :].rearrange("p (c j) -> p c j", c=4),
                                            AX, ALU.max, negate=True).then_inc(max_ready, 1)
                m = n - 1
                if 0 <= m < B:
                    wait(dve, pT_hi_done, m + 1, 1, trip)
                    wait(dve, o_ready, m, 1, trip)
                    nc.vector.tensor_tensor(pT_lo[:, :], pT[:, :], pT_hi[:, :].bitcast(F32),
                                            ALU.subtract).then_inc(pT_lo_done, 1)
                if 0 <= n < B:
                    wait(dve, exp_done, n + 1, 1, trip)
                    wait(dve, probs_ready, n - 1, 1, trip)
                    nc.vector.reciprocal(rsums[:, n % 2, :], sums[:, n % 2, :]).then_inc(rsum_ready, 1)
                g = (n - SPLIT) // GB
                if s == SPLIT % GB and 0 <= g < G:
                    wait(dve, kv_hi_done, g + 1, 1 / GB, trip)
                    wait(dve, o_ready, GB * (g - 1), 1, trip)
                    nc.vector.tensor_tensor(kv_lo[:, g % 2, :, :], kv[:, :, :], kv_hi[:, g % 2, :, :].bitcast(F32),
                                            ALU.subtract).then_inc(kv_lo_done, 1)
                for what, g, sub, bank, count in uses[n]:
                    sh = shared[bank]
                    if what in ("project", "turn_cw", "turn_kv", "query"):
                        continue
                    if what == "turn_x":
                        wait(dve, xT_hi_done, g + 1, 1 / GB, trip)
                        wait(dve, hid1_ready, E * (g - 1), 1, trip)
                        nc.vector.tensor_tensor(xT_lo[:, g % 2, :], sh[:, :], xT_hi[:, g % 2, :].bitcast(F32),
                                                ALU.subtract).then_inc(shared_out[bank], 1)
                    elif what == "residual":
                        wait_shared(dve, shared_full, what, g, sub, trip)
                        wait_shared(dve, shared_out, "finish", g - 2, 2, trip)
                        wait(dve, got_xres, 16 * (g + 1), 16 / GB, trip)
                        nc.vector.tensor_tensor(x1[:, g % 2, :, :], sh[:, :].rearrange("p (c d) -> p c d", c=4),
                                                xres[:, :, :], ALU.add).then_inc(shared_out[bank], 1)
                    elif what == "finish":
                        wait_shared(dve, shared_full, what, g, sub, trip)
                        wait(dve, stored, 16 * g, 16 / GB, trip)
                        nc.vector.scalar_tensor_tensor(out=res[:, :, :], in0=sh[:, :].rearrange("p (c d) -> p c d", c=4),
                                                       scalar=tg[:, 1:2], in1=x1[:, g % 2, :, :],
                                                       op0=ALU.mult, op1=ALU.add).then_inc(shared_out[bank], 1)
                    elif what == "router":
                        wait_shared(dve, shared_full, what, g, sub, trip)
                        nc.vector.tensor_tensor(logit[:, :, :], sh[:, 0:4 * E].rearrange("p (c e) -> p c e", c=4),
                                                br_all[:, :].unsqueeze(1).broadcast_to([P, 4, E]),
                                                ALU.add).then_inc(shared_out[bank], 1)
                g = n // GB + 1
                if s == 3 and 0 <= g < G:
                    wait_shared(dve, shared_out, "turn_kv", g, 1, trip)
                    wait_shared(dve, shared_out, "turn_kv", g, 3, trip)
                    wait_shared(dve, shared_full, "query", g - 1, 6, trip)
                    wait_shared(dve, shared_full, "query", g - 1, 7, trip)
                    nc.vector.tensor_copy(latT_hi[:, :, :], kvT[:, g % 2, :, L:P]).then_inc(latT_done, 1)
                    wait(dve, latT_done, 2 * g + 1, 2 / GB, trip)
                    nc.vector.tensor_tensor(latT_lo[:, :, :], kvT[:, g % 2, :, L:P], latT_hi[:, :, :].bitcast(F32),
                                            ALU.subtract).then_inc(latT_done, 1)
                g = n // GB - 1
                if s == 5 and 0 <= g < G:
                    wait_shared(dve, shared_out, "router", g, 5, trip)
                    nc.vector.tensor_reduce(top[:, :], logit[:, :, :], AX, ALU.max).then_inc(router_step, 1)
                    wait(dve, router_step, 11 * g + 1, 11 / GB, trip)
                    nc.vector.tensor_tensor(shift[:, :, :], logit[:, :, :], top[:, :].unsqueeze(2).broadcast_to([P, 4, E]),
                                            ALU.subtract).then_inc(router_step, 1)
                if s == 3 and 0 <= g < G:
                    wait_shared(dve, shared_out, "residual", g, 2, trip)
                    for c in range(4):
                        last = nc.vector.bn_stats(stats1[:, c, :], x1[:, g % 2, c, :])
                    last.then_inc(stats1_done, 1)
                    count_in_register(dve, g + 1, 1 / GB, trip)
                    dve.wait_ge(const_step, 10)
                    wait(dve, stats1_done, g + 1, 1 / GB, trip)
                    for c in range(4):
                        last = nc.vector.bn_aggr(mv1[:, c, :], stats1[:, c, :])
                    last.then_inc(mv1_done, 1)
                    wait(dve, mv1_done, 2 * g + 1, 2 / GB, trip)
                    nc.vector.tensor_scalar(var_eps1[:, :], mv1[:, :, 1], EPS, None, ALU.add).then_inc(mv1_done, 1)
                g = (n - STATS) // GB
                if s == STATS % GB and 0 <= g < G:
                    wait(dve, got_kv, 32 * (g + 1), 32 / GB, trip)
                    for b in range(GB):
                        last = nc.vector.bn_stats(stats[:, b, :], kv[:, b, :])
                    last.then_inc(stats_done, 1)
                    count_in_register(dve, g + 1, 1 / GB, trip)
                    dve.wait_ge(const_step, 10)
                    wait(dve, stats_done, g + 1, 1 / GB, trip)
                    for b in range(GB):
                        last = nc.vector.bn_aggr(mv[:, b, :], stats[:, b, :])
                    last.then_inc(mv_done, 1)
                    wait(dve, mv_done, 2 * g + 1, 2 / GB, trip)
                    nc.vector.tensor_scalar(var_eps[:, :], mv[:, :, 1], var_mul[:, 0:1], var_add[:, 0:1],
                                            ALU.mult, ALU.add).then_inc(mv_done, 1)
                g = (n - CENTER) // GB
                if s == CENTER % GB and 0 <= g < G:
                    wait(dve, rstd_done, g + 1, 1 / GB, trip)
                    for b in range(GB):
                        last = nc.vector.tensor_scalar(kv[:, b, :], kv[:, b, :], mv[:, b, 0:1], rstd[:, b:b + 1],
                                                       ALU.subtract, ALU.mult)
                    last.then_inc(kv_centered, 1)
                f = expert_of(n)
                if f is not None:
                    wait(dve, hid0_ready, f + 1, 1, trip)
                    wait(dve, got_cw[f % 2], 16 * (f // 2 + 1), 8, trip)
                    wait(dve, ffn_done, f - 1, 1, trip)
                    nc.vector.scalar_tensor_tensor(out=hs[:, f % 2, 0, :], in0=hid[0][:, :],
                                                   scalar=neg_b1[:, 2 * (f % E):2 * (f % E) + 1],
                                                   in1=cw_all[:, f % 2, :], op0=ALU.max, op1=ALU.mult).then_inc(hs0_done, 1)
                g = n // GB - 1
                if s == 3 and 0 <= g < G:
                    wait(dve, rstd1_done, g + 1, 1 / GB, trip)
                    wait_shared(dve, shared_full, "turn_x", g - 1, 4, trip)
                    for c in range(4):
                        last = nc.vector.tensor_scalar(xn[:, c, :], x1[:, g % 2, c, :], mv1[:, c, 0:1], rstd1[:, c:c + 1],
                                                       ALU.subtract, ALU.mult)
                    last.then_inc(xn_done, 1)
                if s == 5 and 0 <= g < G:
                    at = 11 * g
                    wait(dve, rexp_done, g + 1, 1 / GB, trip)
                    nc.vector.tensor_reduce(psumr[:, :], prob[:, :, :], AX, ALU.add).then_inc(router_step, 1)
                    wait(dve, router_step, at + 3, 11 / GB, trip)
                    nc.vector.reciprocal(prec[:, :], psumr[:, :]).then_inc(router_step, 1)
                    wait(dve, router_step, at + 4, 11 / GB, trip)
                    nc.vector.tensor_tensor(probn[:, :, :], prob[:, :, :], prec[:, :].unsqueeze(2).broadcast_to([P, 4, E]),
                                            ALU.mult).then_inc(router_step, 1)
                    wait(dve, router_step, at + 5, 11 / GB, trip)
                    of_f = probn[:, :, :].unsqueeze(2).broadcast_to([P, 4, E, E])
                    of_e = probn[:, :, :].unsqueeze(3).broadcast_to([P, 4, E, E])
                    nc.vector.tensor_tensor(gt[:, :, :, :], of_f, of_e, ALU.is_gt).then_inc(router_step, 1)
                    nc.vector.tensor_tensor(eq[:, :, :, :], of_f, of_e, ALU.is_equal).then_inc(router_step, 1)
                    wait(dve, router_step, at + 7, 11 / GB, trip)
                    nc.vector.tensor_tensor(eqb[:, :, :, :], eq[:, :, :, :], before[:, :, :].unsqueeze(1).broadcast_to([P, 4, E, E]),
                                            ALU.mult).then_inc(router_step, 1)
                    wait(dve, router_step, at + 8, 11 / GB, trip)
                    nc.vector.tensor_tensor(eq[:, :, :, :], gt[:, :, :, :], eqb[:, :, :, :], ALU.add).then_inc(router_step, 1)
                    wait(dve, router_step, at + 9, 11 / GB, trip)
                    nc.vector.tensor_reduce(rank[:, :, :], eq[:, :, :, :], AX, ALU.add).then_inc(router_step, 1)
                    wait(dve, router_step, at + 10, 11 / GB, trip)
                    wait_shared(dve, shared_full, "turn_cw", g - 1, 6, trip)
                    nc.vector.scalar_tensor_tensor(out=cw[:, :, :], in0=rank[:, :, :], scalar=2.0, in1=probn[:, :, :],
                                                   op0=ALU.is_lt, op1=ALU.mult).then_inc(router_step, 1)

            slots(dve, slot)

        @block.tensor
        def _(pe):
            def three_passes(bank, w_hi_, w_lo_, m_hi, m_lo, start=True, stop=True):
                nc.tensor.matmul(bank, w_hi_, m_hi, start=start, stop=False)
                nc.tensor.matmul(bank, w_hi_, m_lo, start=False, stop=False)
                return nc.tensor.matmul(bank, w_lo_, m_hi, start=False, stop=stop)

            pe.wait_ge(got_rows, 16 * 4)
            pe.wait_ge(const_step, 10)
            nc.tensor.transpose(shared[0][:, 0:NR], rows[:, :], ident[0:NR, 0:NR]).then_inc(cols_turned, 1)
            pe.wait_ge(got_attn_w, 16 * 3)
            pe.wait_ge(cols_ready, 1)
            for h in range(H):
                one, two = hid[h % 2], [pT, o][h % 2]
                if h >= 2:
                    pe.wait_ge(w_out, h - 1)
                for k, w in enumerate((Wq_in[:, h * D:(h + 1) * D], Wkv_in[:, h * D:(h + 1) * D],
                                       Wkv_in[:, (H + h) * D:(H + h + 1) * D])):
                    last = nc.tensor.transpose(one[:, k * P:(k + 1) * P], w, ident[:, :])
                last.then_inc(w_turned, 1)
                pe.wait_ge(w_copied, h + 1)
                WqT, WkT, WvT = (wT[:, h % 2, k * P:(k + 1) * P] for k in range(3))
                nc.tensor.matmul(two[:, 0:D], WqT, WkT, start=True, stop=True)
                nc.tensor.matmul(two[:, D:2 * D], WvT, Wo_in[:, h, :], start=True, stop=True)
                nc.tensor.matmul(two[:, 2 * D:2 * D + 1], WkT, cols[:, h:h + 1], start=True, stop=True).then_inc(w_folded, 1)
            for h in range(H):
                last = nc.tensor.matmul(scores[:, 0:1], Wo_in[:, h, :], cols[:, H + h:H + h + 1],
                                        start=(h == 0), stop=(h == H - 1))
            last.then_inc(bias_folded, 1)
            pe.wait_ge(diag_ready, 2)
            pe.wait_ge(got_ffn_w, 16 * 3)
            for e in range(E):
                last = nc.tensor.matmul(shared[1][0:E, 0:D], b1_diag[:, e, :], W2_sb[:, e, 0, :],
                                        start=(e == 0), stop=(e == E - 1))
            last.then_inc(bias_folded, 1)
            pe.wait_ge(bias_ready, 4)
            pe.wait_ge(ffn_ready, 1)

            def slot(n, trip):
                if 0 <= n < B:
                    g, b = n // GB, n % GB
                    if b == 0:
                        wait_shared(pe, shared_out, "query", g, 6, trip)
                        wait_shared(pe, shared_out, "query", g, 7, trip)
                    wait(pe, exp_done, n, 1, trip)
                    for c in range(4):
                        last = nc.tensor.matmul(scores[:, c * P:(c + 1) * P],
                                                qT[:, g % 2, b, 2 * c:2 * c + 2, :].rearrange("p h i -> p (h i)"),
                                                kvT[:, g % 2, b, :], start=True, stop=True)
                    last.then_inc(scores_ready, 1)
                m = n - 1
                if 0 <= m < B:
                    wait(pe, probs_ready, m + 1, 1, trip)
                    wait(pe, pT_lo_done, m, 1, trip)
                    for c in range(4):
                        last = nc.tensor.transpose(pT[:, c * P:(c + 1) * P], probs[:, m % 2, c * P:(c + 1) * P], ident[:, :])
                    last.then_inc(pT_ready, 1)
                f = expert_of(n - 2)
                if f is not None:
                    g, e = f // E, f % E
                    if e == 0:
                        wait(pe, f_done, g, 1 / GB, trip)
                        wait_shared(pe, shared_out, "turn_cw", g, 6, trip)
                        nc.tensor.matmul(acc[:, :], B2[:, :], cwT[:, :], start=True, stop=False)
                    wait(pe, hs0_done, f + 1, 1, trip)
                    nc.tensor.matmul(acc[:, :], W2_sb[:, e, 0, :], hs[:, f % 2, 0, :], start=False, stop=False)
                    wait(pe, hs1_done, f + 1, 1, trip)
                    nc.tensor.matmul(acc[:, :], W2_sb[:, e, 1, :], hs[:, f % 2, 1, :], start=False,
                                     stop=(e == E - 1)).then_inc(ffn_done, 1)
                for what, g, sub, bank, count in uses[n]:
                    sh = shared[bank]
                    if count > 0:
                        pe.wait_ge(shared_out[bank], count + trip * shared_per_trip)
                    if what == "turn_kv":
                        wait(pe, kv_affine, 8 * g + 2 * sub + 2, 8 / GB, trip)
                        for i in range(2):
                            last = nc.tensor.transpose(sh[:, i * P:(i + 1) * P], kv[:, 2 * sub + i, :], ident[:, :])
                    elif what == "query":
                        if sub == 0:
                            wait(pe, latT_done, 2 * (g + 1), 2 / GB, trip)
                        last = three_passes(sh[:, :].rearrange("p (b i) -> p b i", b=GB), A_hi[:, sub, :], A_lo[:, sub, :],
                                            latT_hi[:, :, :], latT_lo[:, :, :])
                    elif what == "project":
                        wait(pe, o_out, GB * (g + 1), 1, trip)
                        for h in range(H):
                            last = nc.tensor.matmul(sh[:, :], M[:, h, :], oT[:, h, :], start=(h == 0), stop=(h == H - 1))
                    elif what == "residual":
                        wait_shared(pe, shared_out, "project", g, 1, trip)
                        for c in range(4):
                            last = nc.tensor.transpose(sh[:, c * P:(c + 1) * P], yT[:, c * P:(c + 1) * P], ident[:, :])
                    elif what == "turn_x":
                        wait(pe, xn_done, g + 1, 1 / GB, trip)
                        for c in range(4):
                            last = nc.tensor.transpose(sh[:, c * P:(c + 1) * P], xn[:, c, :], ident[:, :])
                    elif what == "router":
                        wait_shared(pe, shared_out, "turn_x", g, 4, trip)
                        for c in range(4):
                            rows_c = slice(c * P, (c + 1) * P)
                            last = three_passes(sh[:, c * E:(c + 1) * E], xT_hi[:, g % 2, rows_c], xT_lo[:, g % 2, rows_c],
                                                Wr_hi[:, :], Wr_lo[:, :])
                    elif what == "turn_cw":
                        wait(pe, router_step, 11 * (g + 1), 11 / GB, trip)
                        for c in range(4):
                            last = nc.tensor.transpose(sh[0:E, c * P:(c + 1) * P], cw[:, c, :], ident[:, :])
                    elif what == "finish":
                        wait(pe, f_done, g + 1, 1 / GB, trip)
                        for c in range(4):
                            last = nc.tensor.transpose(sh[:, c * P:(c + 1) * P], fT[:, c * P:(c + 1) * P], ident[:, :])
                    last.then_inc(shared_full[bank], 1)
                f = expert_of(n)
                if f is not None:
                    g, e = f // E, f % E
                    if e == 0:
                        wait_shared(pe, shared_out, "turn_x", g, 4, trip)
                    for c, (done, ready) in enumerate(((hs0_done, hid0_ready), (relu_done, hid1_ready))):
                        wait(pe, done, f, 1, trip)
                        three_passes(hid[c][:, :], W1_hi[:, e, c, :], W1_lo[:, e, c, :],
                                     xT_hi[:, g % 2, :], xT_lo[:, g % 2, :]).then_inc(ready, 1)
                if 0 <= m < B:
                    wait(pe, pT_lo_done, m + 1, 1, trip)
                    wait(pe, kv_lo_done, m // GB + 1, 1 / GB, trip)
                    wait(pe, o_out, m, 1, trip)
                    g, b = m // GB, m % GB
                    three_passes(o[:, :], kv_hi[:, g % 2, b, :], kv_lo[:, g % 2, b, :],
                                 pT_hi[:, :], pT_lo[:, :]).then_inc(o_ready, 1)

            slots(pe, slot)


_INS = ['x', 'ctx_1024', 'g_xattn', 'g_ffn', 'L0_xattn_gamma_media', 'L0_xattn_beta_media', 'L0_xattn_gamma_lat',
        'L0_xattn_beta_lat', 'L0_xattn_Wq', 'L0_xattn_bq', 'L0_xattn_Wkv', 'L0_xattn_bkv', 'L0_xattn_Wo',
        'L0_xattn_bo', 'L0_ffn_Wr', 'L0_ffn_br', 'L0_ffn_W1', 'L0_ffn_b1', 'L0_ffn_W2', 'L0_ffn_b2']
_OUTS = [((B, L, D), 'float32')]


def kernel(**inputs):
    import numpy as _np
    import concourse.bacc as _bacc
    from concourse import mybir as _mybir
    from concourse.bass_utils import run_bass_kernel_spmd as _run

    nc = _bacc.Bacc("TRN2", target_bir_lowering=False, num_devices=1)
    arrays, args = {}, []
    for name in _INS:
        a = _np.ascontiguousarray(inputs[name])
        arrays[f"in_{name}_dram"] = a
        args.append(nc.dram_tensor(f"in_{name}_dram", a.shape, _mybir.dt.from_np(a.dtype), kind="ExternalInput").ap())
    for i, (shape, dtype) in enumerate(_OUTS):
        dt = _mybir.dt.from_np(_np.dtype(dtype))
        args.append(nc.dram_tensor(f"out_{i}_dram", shape, dt, kind="ExternalOutput").ap())
    flamingo(nc, *args)
    r = _run(nc, [arrays], core_ids=[0])
    got = tuple(r.results[0][f"out_{i}_dram"] for i in range(len(_OUTS)))
    return got[0]
```

```python
from contextlib import ExitStack

import concourse.bass as bass
from concourse import mybir

F32 = mybir.dt.float32
F32R = mybir.dt.float32r
ALU = mybir.AluOpType
ACT = mybir.ActivationFunctionType
AX = mybir.AxisListType.X

P = 128
D = 128
B = 128
L = 64
H = 8
E = 8
GB = 8
G = B // GB
TOK = GB * L
EPS = 1e-5
SCALE = float(D) ** -0.5

LOAD = -14
STATS = (-13, -12)
NORMALISE = (-10, -9, -8, -8)
SPLIT = -7
FOLD = {-8: (0, 1), -6: (2, 3), -5: (4,), -4: (5,), -3: (6,), -2: (7,)}
FOLD_FROM, FOLD_BIAS = -8, -1
SPLIT_EXPERTS, FOLD_B1 = range(2, 10), 4
FFN = 15
FIRST, LAST = LOAD, GB * (G - 1) + 25
PER_TRIP = 2 * GB
LOOP_AT, TRIPS = 32, 5

SHARED = {
    0: [("turn_kv", 1, 0, "a")],
    1: [("project", -1, 0, "ab"), ("turn_kv", 1, 1, "a"), ("finish", -3, 0, "c")],
    2: [("residual", -1, 0, "a"), ("query", 1, 0, "b"), ("query", 1, 1, "c")],
    3: [("query", 1, 2, "a"), ("query", 1, 3, "b")],
    4: [("turn_x", -1, 0, "a"), ("query", 1, 4, "b"), ("router", -1, 0, "c")],
    5: [("query", 1, 5, "b")],
    6: [("query", 1, 6, "a"), ("turn_cw", -1, 0, "b")],
    7: [("query", 1, 7, "a")],
}


def plan_shared():
    uses, used = {}, [0, 0]
    for n in range(FIRST, LAST + 1):
        g, s = n // GB, n % GB
        at = sum(len(SHARED[t]) for t in range(s))
        uses[n] = []
        for k, (what, off, number, places) in enumerate(SHARED[s]):
            bank = (at + k) % 2
            if 0 <= g + off < G:
                uses[n].append((what, g + off, number, places, bank, used[bank]))
                used[bank] += 1
    return uses


def flamingo(nc, x, ctx_in, g_xattn, g_ffn, gamma_m, beta_m, gamma_l, beta_l, Wq, bq, Wkv, bkv, Wo, bo,
             Wr, br, W1, b1, W2, b2, out):
    uses = plan_shared()
    use_at = {(what, g, number): (bank, before) for n in uses for what, g, number, _, bank, before in uses[n]}
    shared_per_trip = sum(len(v) for v in SHARED.values())

    ctx = ExitStack()
    with ctx:
        def sb(name, shape, dt=F32):
            return ctx.enter_context(nc.sbuf_tensor(name, shape, dt))

        def psum(name):
            return ctx.enter_context(nc.psum_tensor(name, [P, 512], F32))

        def sem(name):
            return ctx.enter_context(nc.semaphore(name))

        kv = sb("kv", [P, GB, D])
        kv_hi = sb("kv_hi", [P, 2, GB, D], F32R)
        kv_lo = sb("kv_lo", [P, 2, GB, D], F32R)
        kvT = sb("kvT", [P, 2, GB, P])
        latT_hi = sb("latT_hi", [P, GB, L], F32R)
        latT_lo = sb("latT_lo", [P, GB, L], F32R)
        qT = sb("qT", [P, 2, GB, H, L])
        probs = sb("probs", [P, 2, 512])
        pT_hi = sb("pT_hi", [P, 512], F32R)
        pT_lo = sb("pT_lo", [P, 512], F32R)
        oT_hi = sb("oT_hi", [P, H, TOK], F32R)
        oT_lo = sb("oT_lo", [P, H, TOK], F32R)
        yT = sb("yT", [P, TOK])
        fT = sb("fT", [P, TOK])
        xres = sb("xres", [P, 4, D])
        late = sb("late", [P, 8 * TOK])
        W1_in, W2_in = late[:, 0:4 * TOK], late[:, 4 * TOK:8 * TOK]
        hs = late[:, 0:2 * TOK].rearrange("p (c n) -> p c n", c=2)
        cw_all = late[:, 2 * TOK:4 * TOK].rearrange("p (a n) -> p a n", a=2)
        x1 = late[:, 4 * TOK:6 * TOK].rearrange("p (a c d) -> p a c d", a=2, c=4)
        hr = late[:, 6 * TOK:7 * TOK]
        tokens = late[:, 7 * TOK:8 * TOK].rearrange("p (c d) -> p c d", c=4)
        xn = res = tokens
        xT_hi = sb("xT_hi", [P, 2, TOK], F32R)
        xT_lo = sb("xT_lo", [P, 2, TOK], F32R)
        cwT = sb("cwT", [E, TOK])
        hs_hi = sb("hs_hi", [P, 2, 2, TOK], F32R)
        hs_lo = sb("hs_lo", [P, 2, 2, TOK], F32R)
        AM_hi = sb("AM_hi", [P, H, 2, D], F32R)
        AM_lo = sb("AM_lo", [P, H, 2, D], F32R)
        W1_hi = sb("W1_hi", [P, E, 2, P], F32R)
        W1_lo = sb("W1_lo", [P, E, 2, P], F32R)
        W2_hi = sb("W2_hi", [P, E, 2, D], F32R)
        W2_lo = sb("W2_lo", [P, E, 2, D], F32R)
        Wr_f = sb("Wr_f", [P, E])
        Wr_hi = sb("Wr_hi", [P, E], F32R)
        Wr_lo = sb("Wr_lo", [P, E], F32R)
        NR = 2 * H + 2 * E + 1
        rows = sb("rows", [NR, D])
        cols = sb("cols", [P, NR])
        tb = sb("tb", [P, H])
        neg_b1 = sb("neg_b1", [P, 2 * E])
        b1_diag = sb("b1_diag", [P, E, E])
        b2_f = sb("b2_f", [E, D])
        B2 = sb("B2", [E, D])
        gamma = sb("gamma", [P, D])
        beta = sb("beta", [P, D])
        br_all = sb("br_all", [P, E])
        gates = sb("gates", [P, 2])
        tg = sb("tg", [P, 2])
        bo_sum = sb("bo_sum", [P, 1])
        tg_bo = sb("tg_bo", [P, 1])
        ident = sb("ident", [P, P])
        ones_sq = yT[:, 0:P]
        before = sb("before", [P, E, E])
        neg_half = sb("neg_half", [P, GB])
        ones_col = sb("ones_col", [P, 2])
        var_mul = sb("var_mul", [P, 1])
        var_add = sb("var_add", [P, 1])
        stats = sb("stats", [P, GB, 6])
        mv = sb("mv", [P, GB, 2])
        rstd = sb("rstd", [P, GB])
        var_eps = sb("var_eps", [P, GB])
        neg_max = sb("neg_max", [P, 2, 4])
        sums = sb("sums", [P, 2, 4])
        rsums = sb("rsums", [P, 2, 4])
        stats1 = sb("stats1", [P, 4, 6])
        mv1 = sb("mv1", [P, 4, 2])
        var_eps1 = sb("var_eps1", [P, 4])
        rstd1 = sb("rstd1", [P, 4])
        logit = sb("logit", [P, 4, E])
        shift = sb("shift", [P, 4, E])
        prob = sb("prob", [P, 4, E])
        probn = sb("probn", [P, 4, E])
        top = sb("top", [P, 4])
        psumr = sb("psumr", [P, 4])
        prec = sb("prec", [P, 4])
        gt = sb("gt", [P, 4, E, E])
        eq = sb("eq", [P, 4, E, E])
        rank = sb("rank", [P, 4, E])
        cw = sb("cw", [P, 4, E])
        staged = qT[:, 1, :, :, :].rearrange("p b h i -> p (b h i)")
        Wq_in, Wkv_in = staged[:, 0:H * D], staged[:, H * D:3 * H * D]
        Wo_in = staged[:, 3 * H * D:4 * H * D].rearrange("p (h n) -> p h n", h=H)
        wT = probs

        scores = psum("scores")
        pT = psum("pT")
        o = psum("o")
        hid = [psum("hid0"), psum("hid1")]
        acc = psum("acc")
        shared = [psum("shared0"), psum("shared1")]

        cw_dram = nc.dram_tensor("cw_rows", (2, E, TOK), F32).ap()

        got_rows = sem("got_rows")
        got_attn_w = [sem("got_attn_w0"), sem("got_attn_w1")]
        got_ffn_w = sem("got_ffn_w")
        got_small = sem("got_small")
        got_kv = sem("got_kv")
        got_xres = sem("got_xres")
        const_step = sem("const_step")
        gates_done = sem("gates_done")
        cols_turned = sem("cols_turned")
        cols_ready = sem("cols_ready")
        w_turned = sem("w_turned")
        w_copied = sem("w_copied")
        w_folded = sem("w_folded")
        w_hi = sem("w_hi")
        w_lo = sem("w_lo")
        bias_folded = sem("bias_folded")
        bias_ready = sem("bias_ready")
        diag_ready = sem("diag_ready")
        ffn_hi = sem("ffn_hi")
        ffn_ready = sem("ffn_ready")
        wr_ready = sem("wr_ready")
        stats_done = sem("stats_done")
        mv_done = sem("mv_done")
        rstd_done = sem("rstd_done")
        kv_scaled = sem("kv_scaled")
        kv_ready = sem("kv_ready")
        kv_hi_done = sem("kv_hi_done")
        kv_lo_done = sem("kv_lo_done")
        scores_ready = sem("scores_ready")
        max_ready = sem("max_ready")
        exp_done = sem("exp_done")
        rsum_ready = sem("rsum_ready")
        probs_ready = sem("probs_ready")
        pT_ready = sem("pT_ready")
        pT_hi_done = sem("pT_hi_done")
        pT_lo_done = sem("pT_lo_done")
        o_ready = sem("o_ready")
        o_hi_done = sem("o_hi_done")
        o_out = sem("o_out")
        stats1_done = sem("stats1_done")
        mv1_done = sem("mv1_done")
        rstd1_done = sem("rstd1_done")
        xn_done = sem("xn_done")
        router_step = sem("router_step")
        rexp_done = sem("rexp_done")
        cw_stored = sem("cw_stored")
        got_cw = [sem("got_cw_even"), sem("got_cw_odd")]
        hid0_ready = sem("hid0_ready")
        hid1_ready = sem("hid1_ready")
        hs0_done = sem("hs0_done")
        relu_done = sem("relu_done")
        hs1_done = sem("hs1_done")
        hs0_hi_done = sem("hs0_hi_done")
        hs0_lo_done = sem("hs0_lo_done")
        hs1_hi_done = sem("hs1_hi_done")
        hs1_lo_done = sem("hs1_lo_done")
        ffn_done = sem("ffn_done")
        f_done = sem("f_done")
        stored = sem("stored")
        shared_full = [sem("shared_full0"), sem("shared_full1")]
        shared_out = [sem("shared_out0"), sem("shared_out1")]
        latT_done = sem("latT_done")
        xT_hi_done = sem("xT_hi_done")

        def slots(eng, body, weights):
            for n in range(FIRST, LOOP_AT):
                weights(n)
                body(n, 0)
            with eng.Fori(0, TRIPS) as trip:
                for n in range(LOOP_AT, LOOP_AT + PER_TRIP):
                    body(n, trip)
            for n in range(LOOP_AT + PER_TRIP * TRIPS, LAST + 1):
                body(n, 0)

        def wait(eng, s, value, per_slot, trip):
            if value > 0:
                eng.wait_ge(s, value + trip * int(per_slot * PER_TRIP))

        def wait_shared(eng, sems, what, g, number, trip):
            if (what, g, number) in use_at:
                bank, count = use_at[what, g, number]
                eng.wait_ge(sems[bank], count + 1 + trip * shared_per_trip)

        def shared_at(n, place, reader):
            on_dve = ("finish", "residual", "router")
            return [(what, g, number, bank) for what, g, number, places, bank, _ in uses[n]
                    if places[-1] == place and (what in on_dve) == (reader == "dve")]

        def count_in_register(eng, value, per_slot, trip):
            if not isinstance(trip, int):
                eng.compute_val(value + trip * int(per_slot * PER_TRIP))

        def first_row(eng, g, trip):
            return g * GB if isinstance(trip, int) else eng.snap((g + 2 * trip) * GB)

        def expert_of(n):
            f = n - FFN
            return f if 0 <= f < G * E else None

        block = ctx.enter_context(nc.Block())

        @block.sync
        def _(sp):
            def weights(n):
                if n == FIRST + 1:
                    sp.dma_start(rows[0:H, :], bq.rearrange("(h d) -> h d", h=H)).then_inc(got_rows, 16)
                    sp.dma_start(rows[H:2 * H, :], bkv[H * D:2 * H * D].rearrange("(h d) -> h d", h=H)).then_inc(got_rows, 16)
                    sp.dma_start(rows[2 * H:2 * H + 2 * E, :], b1.rearrange("e (c f) -> (e c) f", c=2)).then_inc(got_rows, 16)
                    sp.dma_start(rows[NR - 1:NR, :], bo.rearrange("(a n) -> a n", a=1)).then_inc(got_rows, 16)
                    for half in range(2):
                        w = slice(half * (H // 2) * D, (half + 1) * (H // 2) * D)
                        heads = slice(half * (H // 2), (half + 1) * (H // 2))
                        sp.dma_start(Wq_in[:, w], Wq[:, w]).then_inc(got_attn_w[half], 16)
                        sp.dma_start(Wkv_in.rearrange("p (t n) -> p t n", t=2)[:, :, w],
                                     Wkv.rearrange("p (t n) -> p t n", t=2)[:, :, w]).then_inc(got_attn_w[half], 16)
                        sp.dma_start(Wo_in[:, heads, :], Wo[w, :].rearrange("(h e) n -> e h n", h=H // 2)).then_inc(got_attn_w[half], 16)

            def slot(n, trip):
                s = n % GB
                g = (n - LOAD) // GB
                if s == LOAD % GB and 0 <= g < G:
                    at = bass.ds(first_row(sp, g, trip), GB)
                    count_in_register(sp, 2 * g, 2 / GB, trip)
                    count_in_register(sp, g, 1 / GB, trip)
                    wait(sp, latT_done, 2 * g, 2 / GB, trip)
                    wait(sp, kv_lo_done, g, 1 / GB, trip)
                    sp.dma_start(kv[0:L, :, :], ctx_in[at, :, :].rearrange("b s d -> s b d")).then_inc(got_kv, 16)
                    sp.dma_start(kv[L:P, :, :], x[at, :, :].rearrange("b s d -> s b d")).then_inc(got_kv, 16)
                g = n // GB
                if s == 4 and 0 <= g < G:
                    at = bass.ds(first_row(sp, g, trip), GB)
                    wait_shared(sp, shared_out, "residual", g - 1, 0, trip)
                    sp.dma_start(xres[:, :, :], x[at, :, :].rearrange("(c b) s d -> (b s) c d", b=2)).then_inc(got_xres, 16)
                g = n // GB - 1
                if s == 6 and 0 <= g < G:
                    count_in_register(sp, 8 * E * (g - 1), 8, trip)
                    wait_shared(sp, shared_out, "turn_cw", g, 0, trip)
                    wait(sp, got_cw[0], 8 * E * (g - 1), 8, trip)
                    wait(sp, got_cw[1], 8 * E * (g - 1), 8, trip)
                    sp.dma_start(cw_dram[g % 2, :, :], cwT[:, :]).then_inc(cw_stored, 16)
                f = expert_of(n + 1)
                if f is not None:
                    stored_count, used_count = 16 * (f // E + 1) + trip * 32, f - 1 + trip * PER_TRIP
                    count_in_register(sp, 16 * (f // E + 1), 16 / GB, trip)
                    count_in_register(sp, f - 1, 1, trip)
                    sp.wait_ge(cw_stored, stored_count)
                    if f > 1:
                        sp.wait_ge(hs0_done, used_count)
                        sp.wait_ge(hs1_done, used_count)
                    sp.dma_start(cw_all[:, f % 2, :],
                                 cw_dram[f // E % 2, f % E, :].partition_broadcast(P)).then_inc(got_cw[f % 2], 16)
                g = n // GB - 3
                if s == 1 and 0 <= g < G:
                    at = bass.ds(first_row(sp, g, trip), GB)
                    wait_shared(sp, shared_out, "finish", g, 0, trip)
                    sp.dma_start(out[at, :, :].rearrange("(c b) s d -> (b s) c d", b=2), res[:, :, :]).then_inc(stored, 16)

            slots(sp, slot, weights)
            sp.wait_ge(stored, 16 * G)
            sp.wait_ge(cw_stored, 16 * G)

        @block.gpsimd
        def _(pool):
            nc.gpsimd.memset(neg_half[:, :], -0.5).then_inc(const_step, 1)
            nc.gpsimd.memset(ones_col[:, 0:1], 1.0 + EPS).then_inc(const_step, 1)
            nc.gpsimd.memset(ones_col[:, 1:2], EPS * EPS).then_inc(const_step, 1)
            nc.gpsimd.memset(ones_sq[:, :], 1.0).then_inc(const_step, 1)
            nc.gpsimd.memset(b1_diag[:, :, :], 0.0).then_inc(const_step, 1)
            nc.gpsimd.memset(eq[:, 0, :, :], 1.0).then_inc(const_step, 1)
            pool.wait_ge(const_step, 6)
            nc.gpsimd.affine_select(out=var_mul[:, :], in_=ones_col[:, 0:1], compare_op=ALU.is_ge, fill=1.0,
                                    base=-L, pattern=[[0, 1]], channel_multiplier=1).then_inc(const_step, 1)
            nc.gpsimd.affine_select(out=var_add[:, :], in_=ones_col[:, 1:2], compare_op=ALU.is_ge, fill=EPS,
                                    base=-L, pattern=[[0, 1]], channel_multiplier=1).then_inc(const_step, 1)
            nc.gpsimd.affine_select(out=ident[:, :], in_=ones_sq[:, :], compare_op=ALU.is_equal, fill=0.0,
                                    base=0, pattern=[[-1, P]], channel_multiplier=1).then_inc(const_step, 1)
            nc.gpsimd.affine_select(out=before[:, :, :], in_=eq[:, 0, :, :], compare_op=ALU.is_gt, fill=0.0,
                                    base=0, pattern=[[1, E], [-1, E]], channel_multiplier=0).then_inc(const_step, 1)

            def slot(n, trip):
                s = n % GB
                if 0 <= n < B:
                    wait(pool, rsum_ready, n + 1, 1, trip)
                    pv = probs[:, n % 2, :].rearrange("p (c j) -> p c j", c=4)
                    nc.gpsimd.tensor_tensor(pv, pv, rsums[:, n % 2, :].unsqueeze(2).broadcast_to([P, 4, P]),
                                            ALU.mult).then_inc(probs_ready, 1)
                f = expert_of(n)
                if f is not None:
                    wait(pool, relu_done, f + 1, 1, trip)
                    wait(pool, got_cw[f % 2], 16 * (f // 2 + 1), 8, trip)
                    wait(pool, hs1_lo_done, f, 1, trip)
                    nc.gpsimd.tensor_tensor(hs[:, 1, :], hr[:, :], cw_all[:, f % 2, :], ALU.mult).then_inc(hs1_done, 1)
                    wait(pool, hs1_hi_done, f + 1, 1, trip)
                    nc.gpsimd.tensor_tensor(hs_lo[:, f % 2, 1, :], hs[:, 1, :], hs_hi[:, f % 2, 1, :].bitcast(F32),
                                            ALU.subtract).then_inc(hs1_lo_done, 1)
                g = (n - STATS[1]) // GB
                if s == STATS[1] % GB and 0 <= g < G:
                    wait(pool, mv_done, 2 * (g + 1), 2 / GB, trip)
                    nc.gpsimd.tensor_tensor(rstd[:, :], var_eps[:, :], neg_half[:, :], ALU.pow).then_inc(rstd_done, 1)
                g = n // GB - 1
                if s == 2 and 0 <= g < G:
                    wait(pool, mv1_done, 2 * (g + 1), 2 / GB, trip)
                    nc.gpsimd.tensor_tensor(rstd1[:, :], var_eps1[:, :], neg_half[:, 0:4], ALU.pow).then_inc(rstd1_done, 1)

            def weights(n):
                e = n - 1 - SPLIT_EXPERTS[0]
                if 0 <= e < E:
                    pool.wait_ge(ffn_hi, 2 * (e + 1))
                    nc.gpsimd.tensor_tensor(W1_lo[:, e, :, :].rearrange("p c f -> p (c f)"), W1_in[:, e * 2 * P:(e + 1) * 2 * P],
                                            W1_hi[:, e, :, :].rearrange("p c f -> p (c f)").bitcast(F32), ALU.subtract)
                    nc.gpsimd.tensor_tensor(W2_lo[:, e, :, :].rearrange("p c n -> p (c n)"), W2_in[:, e * 2 * D:(e + 1) * 2 * D],
                                            W2_hi[:, e, :, :].rearrange("p c n -> p (c n)").bitcast(F32),
                                            ALU.subtract).then_inc(ffn_ready, 1)

            slots(pool, slot, weights)

        @block.scalar
        def _(act):
            act.dma_start(gamma[0:L, :], gamma_m.partition_broadcast(L)).then_inc(got_small, 16)
            act.dma_start(gamma[L:P, :], gamma_l.partition_broadcast(L)).then_inc(got_small, 16)
            act.dma_start(beta[0:L, :], beta_m.partition_broadcast(L)).then_inc(got_small, 16)
            act.dma_start(beta[L:P, :], beta_l.partition_broadcast(L)).then_inc(got_small, 16)
            act.dma_start(gates[:, 0:1], g_xattn.partition_broadcast(P)).then_inc(got_small, 16)
            act.dma_start(gates[:, 1:2], g_ffn.partition_broadcast(P)).then_inc(got_small, 16)
            act.dma_start(br_all[:, :], br.partition_broadcast(P)).then_inc(got_small, 16)
            act.dma_start(b2_f[:, :], b2).then_inc(got_small, 16)

            def copy_turned(h):
                act.wait_ge(w_turned, h + 1)
                if h >= 2:
                    act.wait_ge(w_folded, h - 1)
                nc.scalar.activation(wT[:, h % 2, 0:3 * P], hid[h % 2][:, 0:3 * P], ACT.Copy).then_inc(w_copied, 1)

            def weights(n):
                if n == FOLD_FROM:
                    act.wait_ge(got_small, 16 * 8)
                    nc.scalar.activation(tg[:, :], gates[:, :], ACT.Tanh).then_inc(gates_done, 1)
                    act.wait_ge(cols_turned, 1)
                    nc.scalar.activation(cols[:, :], acc[:, 0:NR], ACT.Copy).then_inc(cols_ready, 1)
                    copy_turned(0)
                for h in FOLD.get(n, ()):
                    if h + 1 < H:
                        copy_turned(h + 1)
                    act.wait_ge(w_folded, h + 1)
                    nc.scalar.activation(AM_hi[:, h, :, :].rearrange("p a n -> p (a n)"), [pT, o][h % 2][:, 0:2 * D],
                                         ACT.Copy).then_inc(w_hi, 1)
                if n == FOLD_BIAS:
                    act.dma_start(W1_in.rearrange("p (e f) -> p e f", e=E), W1.rearrange("e d f -> d e f")).then_inc(got_ffn_w, 16)
                    act.dma_start(W2_in.rearrange("p (e c n) -> p e c n", e=E, c=2), W2.rearrange("e (c f) n -> f e c n", c=2)).then_inc(got_ffn_w, 16)
                    act.dma_start(Wr_f[:, :], Wr).then_inc(got_ffn_w, 16)
                if n == SPLIT_EXPERTS[0] + 1:
                    act.wait_ge(got_ffn_w, 16 * 3)
                e = n - 1 - SPLIT_EXPERTS[0]
                if 0 <= e < E:
                    nc.scalar.activation(W1_hi[:, e, :, :].rearrange("p c f -> p (c f)"), W1_in[:, e * 2 * P:(e + 1) * 2 * P],
                                         ACT.Copy).then_inc(ffn_hi, 1)
                    nc.scalar.activation(W2_hi[:, e, :, :].rearrange("p c n -> p (c n)"), W2_in[:, e * 2 * D:(e + 1) * 2 * D],
                                         ACT.Copy).then_inc(ffn_hi, 1)
                if e == E - 1:
                    nc.scalar.activation(Wr_hi[:, :], Wr_f[:, :], ACT.Copy).then_inc(ffn_hi, 1)

            def slot(n, trip):
                s = n % GB
                m = n - 1
                if 0 <= m < B:
                    wait(act, pT_ready, m + 1, 1, trip)
                    wait(act, o_ready, m, 1, trip)
                    nc.scalar.activation(pT_hi[:, :], pT[:, :], ACT.Copy).then_inc(pT_hi_done, 1)
                g = n // GB - 1
                if s == 5 and 0 <= g < G:
                    wait(act, router_step, 11 * g + 2, 11 / GB, trip)
                    nc.scalar.activation(prob[:, :, :], shift[:, :, :], ACT.Exp).then_inc(rexp_done, 1)
                g = n // GB - 3
                if s == 0 and 0 <= g < G:
                    wait(act, ffn_done, E * (g + 1), 1, trip)
                    wait_shared(act, shared_full, "finish", g - 1, 0, trip)
                    nc.scalar.activation(fT[:, :], acc[:, :], ACT.Copy).then_inc(f_done, 1)
                if 0 <= n < B:
                    wait(act, max_ready, n + 1, 1, trip)
                    wait(act, pT_ready, n - 1, 1, trip)
                    wait(act, rsum_ready, n - 1, 1, trip)
                    for c in range(4):
                        last = nc.scalar.activation(probs[:, n % 2, c * P:(c + 1) * P], scores[:, c * P:(c + 1) * P],
                                                    ACT.Exp, bias=neg_max[:, n % 2, c:c + 1],
                                                    accum_out=sums[:, n % 2, c:c + 1])
                    last.then_inc(exp_done, 1)
                if s == 6:
                    read_out(n, "b", trip)
                read_out(n, "a", trip)
                f = expert_of(n)
                if f is not None:
                    wait(act, hid1_ready, f + 1, 1, trip)
                    wait(act, hs1_done, f, 1, trip)
                    nc.scalar.activation(hr[:, :], hid[1][:, :], ACT.Relu,
                                         bias=cols[:, 2 * H + 2 * (f % E) + 1:2 * H + 2 * (f % E) + 2]).then_inc(relu_done, 1)
                    wait(act, hs0_done, f + 1, 1, trip)
                    wait(act, ffn_done, f - 1, 1, trip)
                    nc.scalar.activation(hs_hi[:, f % 2, 0, :], hs[:, 0, :], ACT.Copy).then_inc(hs0_hi_done, 1)
                if s != 6:
                    read_out(n, "b", trip)
                if 0 <= m < B:
                    wait(act, o_ready, m + 1, 1, trip)
                    if m % GB == 0:
                        wait_shared(act, shared_full, "project", m // GB - 1, 0, trip)
                    b = m % GB
                    nc.scalar.activation(oT_hi[:, :, b * L:(b + 1) * L], o[:, :].rearrange("p (h i) -> p h i", h=H),
                                         ACT.Copy).then_inc(o_hi_done, 1)
                g = (n - SPLIT) // GB
                if s == SPLIT % GB and 0 <= g < G:
                    wait(act, kv_ready, 4 * (g + 1), 4 / GB, trip)
                    wait(act, o_ready, GB * (g - 1), 1, trip)
                    nc.scalar.activation(kv_hi[:, g % 2, :, :], kv[:, :, :], ACT.Copy).then_inc(kv_hi_done, 1)
                if f is not None:
                    wait(act, hs1_done, f + 1, 1, trip)
                    nc.scalar.activation(hs_hi[:, f % 2, 1, :], hs[:, 1, :], ACT.Copy).then_inc(hs1_hi_done, 1)
                read_out(n, "c", trip)

            def read_out(n, place, trip):
                for what, g, number, bank in shared_at(n, place, "act"):
                    sh = shared[bank]
                    wait_shared(act, shared_full, what, g, number, trip)
                    if what == "turn_kv":
                        wait(act, scores_ready, GB * (g - 1), 1, trip)
                        nc.scalar.activation(kvT[:, g % 2, 4 * number:4 * number + 4, :].rearrange("p b j -> p (b j)"),
                                             sh[:, :], ACT.Copy).then_inc(shared_out[bank], 1)
                    elif what == "query":
                        wait(act, scores_ready, GB * (g - 1), 1, trip)
                        nc.scalar.activation(qT[:, g % 2, :, number, :], sh[:, :].rearrange("p (b i) -> p b i", b=GB),
                                             ACT.Identity, bias=tb[:, number:number + 1], scale=SCALE).then_inc(shared_out[bank], 1)
                    elif what == "project":
                        wait_shared(act, shared_full, "residual", g - 1, 0, trip)
                        if g == 0:
                            act.wait_ge(bias_ready, 2)
                        nc.scalar.activation(yT[:, :], sh[:, :], ACT.Identity, bias=tg_bo[:, 0:1],
                                             scale=tg[:, 0:1]).then_inc(shared_out[bank], 1)
                    elif what == "turn_x":
                        wait(act, hid1_ready, E * (g - 1), 1, trip)
                        nc.scalar.activation(xT_hi[:, g % 2, :], sh[:, :], ACT.Copy).then_inc(xT_hi_done, 1)
                    elif what == "turn_cw":
                        wait(act, cw_stored, 16 * g, 16 / GB, trip)
                        wait(act, ffn_done, E * (g - 1) + 1, 1, trip)
                        nc.scalar.activation(cwT[:, :], sh[0:E, :], ACT.Copy).then_inc(shared_out[bank], 1)

            slots(act, slot, weights)

        @block.vector
        def _(dve):
            def weights(n):
                if n == NORMALISE[0]:
                    dve.wait_ge(got_small, 16 * 8)
                if n == FOLD_FROM:
                    dve.wait_ge(cols_ready, 1)
                    nc.vector.tensor_scalar(neg_b1[:, :], cols[:, 2 * H:2 * H + 2 * E], -1.0, None, ALU.mult).then_inc(diag_ready, 1)
                    nc.vector.tensor_copy(b1_diag[:, :, :].rearrange("p e f -> p (e f)")[:, 0:E * E:E + 1],
                                          cols[:, 2 * H:2 * H + 2 * E:2]).then_inc(diag_ready, 1)
                for h in FOLD.get(n, ()):
                    bank = [pT, o][h % 2]
                    dve.wait_ge(w_hi, h + 1)
                    nc.vector.tensor_tensor(AM_lo[:, h, :, :].rearrange("p a n -> p (a n)"), bank[:, 0:2 * D],
                                            AM_hi[:, h, :, :].rearrange("p a n -> p (a n)").bitcast(F32), ALU.subtract)
                    nc.vector.tensor_scalar(tb[:, h:h + 1], bank[:, 2 * D:2 * D + 1], SCALE, None, ALU.mult).then_inc(w_lo, 1)
                if n == FOLD_BIAS:
                    dve.wait_ge(bias_folded, 1)
                    nc.vector.tensor_tensor(bo_sum[:, :], acc[:, NR:NR + 1], cols[:, NR - 1:NR], ALU.add).then_inc(bias_ready, 1)
                    dve.wait_ge(bias_ready, 1)
                    dve.wait_ge(gates_done, 1)
                    nc.vector.tensor_tensor(tg_bo[:, :], bo_sum[:, :], tg[:, 0:1], ALU.mult).then_inc(bias_ready, 1)
                if n == FOLD_B1 + 1:
                    dve.wait_ge(bias_folded, 2)
                    nc.vector.tensor_tensor(B2[:, :], hid[1][0:E, 0:D], b2_f[:, :], ALU.add).then_inc(bias_ready, 1)
                if n == SPLIT_EXPERTS[-1] + 1:
                    dve.wait_ge(ffn_hi, 2 * E + 1)
                    nc.vector.tensor_tensor(Wr_lo[:, :], Wr_f[:, :], Wr_hi[:, :].bitcast(F32), ALU.subtract).then_inc(wr_ready, 1)
                    dve.wait_ge(ffn_ready, E)

            def normalise_kv(n, k, trip):
                g = (n - NORMALISE[k]) // GB
                if n % GB == NORMALISE[k] % GB and 0 <= g < G:
                    if k == 0:
                        wait(dve, rstd_done, g + 1, 1 / GB, trip)
                    for b in (2 * k, 2 * k + 1):
                        last = nc.vector.scalar_tensor_tensor(out=kv[:, b, :], in0=kv[:, b, :], scalar=mv[:, b, 0:1],
                                                              in1=gamma[:, :], op0=ALU.subtract, op1=ALU.mult)
                    last.then_inc(kv_scaled, 1)
                    wait(dve, kv_scaled, 4 * g + k + 1, 4 / GB, trip)
                    for b in (2 * k, 2 * k + 1):
                        last = nc.vector.scalar_tensor_tensor(out=kv[:, b, :], in0=kv[:, b, :], scalar=rstd[:, b:b + 1],
                                                              in1=beta[:, :], op0=ALU.mult, op1=ALU.add)
                    last.then_inc(kv_ready, 1)

            def split_latents(n, s, trip):
                g = n // GB + 1
                if s == 1 and 0 <= g < G:
                    wait_shared(dve, shared_out, "turn_kv", g, 1, trip)
                    wait_shared(dve, shared_full, "query", g - 1, 7, trip)
                    nc.vector.tensor_copy(latT_hi[:, :, :], kvT[:, g % 2, :, L:P]).then_inc(latT_done, 1)
                    wait(dve, latT_done, 2 * g + 1, 2 / GB, trip)
                    nc.vector.tensor_tensor(latT_lo[:, :, :], kvT[:, g % 2, :, L:P], latT_hi[:, :, :].bitcast(F32),
                                            ALU.subtract).then_inc(latT_done, 1)

            def split_kv(n, s, trip):
                g = (n - SPLIT) // GB
                if s == SPLIT % GB and 0 <= g < G:
                    wait(dve, kv_hi_done, g + 1, 1 / GB, trip)
                    wait(dve, o_ready, GB * (g - 1), 1, trip)
                    nc.vector.tensor_tensor(kv_lo[:, g % 2, :, :], kv[:, :, :], kv_hi[:, g % 2, :, :].bitcast(F32),
                                            ALU.subtract).then_inc(kv_lo_done, 1)

            def measure_rows(n, s, trip):
                g = n // GB - 1
                if s == 2 and 0 <= g < G:
                    wait_shared(dve, shared_out, "residual", g, 0, trip)
                    for c in range(4):
                        last = nc.vector.bn_stats(stats1[:, c, :], x1[:, g % 2, c, :])
                    last.then_inc(stats1_done, 1)
                    count_in_register(dve, g + 1, 1 / GB, trip)
                    dve.wait_ge(const_step, 10)
                    wait(dve, stats1_done, g + 1, 1 / GB, trip)
                    for c in range(4):
                        last = nc.vector.bn_aggr(mv1[:, c, :], stats1[:, c, :])
                    last.then_inc(mv1_done, 1)
                    wait(dve, mv1_done, 2 * g + 1, 2 / GB, trip)
                    nc.vector.tensor_scalar(var_eps1[:, :], mv1[:, :, 1], EPS, None, ALU.add).then_inc(mv1_done, 1)

            def measure_kv(n, half, trip):
                g = (n - STATS[half]) // GB
                if n % GB == STATS[half] % GB and 0 <= g < G:
                    if half == 0:
                        wait(dve, got_kv, 32 * (g + 1), 32 / GB, trip)
                    for b in range(4 * half, 4 * half + 4):
                        last = nc.vector.bn_stats(stats[:, b, :], kv[:, b, :])
                    last.then_inc(stats_done, 1)

            def aggregate_kv(n, s, trip):
                g = (n - STATS[1]) // GB
                if s == STATS[1] % GB and 0 <= g < G:
                    count_in_register(dve, 2 * (g + 1), 2 / GB, trip)
                    dve.wait_ge(const_step, 10)
                    wait(dve, stats_done, 2 * (g + 1), 2 / GB, trip)
                    for b in range(GB):
                        last = nc.vector.bn_aggr(mv[:, b, :], stats[:, b, :])
                    last.then_inc(mv_done, 1)
                    wait(dve, mv_done, 2 * g + 1, 2 / GB, trip)
                    nc.vector.tensor_scalar(var_eps[:, :], mv[:, :, 1], var_mul[:, 0:1], var_add[:, 0:1],
                                            ALU.mult, ALU.add).then_inc(mv_done, 1)

            def normalise_rows(n, s, trip):
                g = n // GB - 1
                if s == 3 and 0 <= g < G:
                    wait(dve, rstd1_done, g + 1, 1 / GB, trip)
                    wait(dve, stored, 16 * (g - 1), 16 / GB, trip)
                    for c in range(4):
                        last = nc.vector.tensor_scalar(xn[:, c, :], x1[:, g % 2, c, :], mv1[:, c, 0:1], rstd1[:, c:c + 1],
                                                       ALU.subtract, ALU.mult)
                    last.then_inc(xn_done, 1)

            def router_softmax(n, s, trip):
                g = n // GB - 1
                if s == 5 and 0 <= g < G:
                    wait(dve, rexp_done, g + 1, 1 / GB, trip)
                    nc.vector.tensor_reduce(psumr[:, :], prob[:, :, :], AX, ALU.add).then_inc(router_step, 1)
                    wait(dve, router_step, 11 * g + 3, 11 / GB, trip)
                    nc.vector.reciprocal(prec[:, :], psumr[:, :]).then_inc(router_step, 1)
                    wait(dve, router_step, 11 * g + 4, 11 / GB, trip)
                    nc.vector.tensor_tensor(probn[:, :, :], prob[:, :, :], prec[:, :].unsqueeze(2).broadcast_to([P, 4, E]),
                                            ALU.mult).then_inc(router_step, 1)

            def router_compare(n, s, trip):
                g = n // GB - 1
                if s == 5 and 0 <= g < G:
                    wait(dve, router_step, 11 * g + 5, 11 / GB, trip)
                    of_f = probn[:, :, :].unsqueeze(2).broadcast_to([P, 4, E, E])
                    of_e = probn[:, :, :].unsqueeze(3).broadcast_to([P, 4, E, E])
                    nc.vector.tensor_tensor(gt[:, :, :, :], of_f, of_e, ALU.is_gt).then_inc(router_step, 1)
                    nc.vector.tensor_tensor(eq[:, :, :, :], of_f, of_e, ALU.is_equal).then_inc(router_step, 1)
                    wait(dve, router_step, 11 * g + 7, 11 / GB, trip)
                    nc.vector.tensor_tensor(eq[:, :, :, :], eq[:, :, :, :], before[:, :, :].unsqueeze(1).broadcast_to([P, 4, E, E]),
                                            ALU.mult).then_inc(router_step, 1)

            def router_rank(n, s, trip):
                g = n // GB - 1
                if s == 5 and 0 <= g < G:
                    wait(dve, router_step, 11 * g + 8, 11 / GB, trip)
                    nc.vector.tensor_tensor(eq[:, :, :, :], gt[:, :, :, :], eq[:, :, :, :], ALU.add).then_inc(router_step, 1)
                    wait(dve, router_step, 11 * g + 9, 11 / GB, trip)
                    nc.vector.tensor_reduce(rank[:, :, :], eq[:, :, :, :], AX, ALU.add).then_inc(router_step, 1)
                    wait(dve, router_step, 11 * g + 10, 11 / GB, trip)
                    wait_shared(dve, shared_full, "turn_cw", g - 1, 0, trip)
                    nc.vector.scalar_tensor_tensor(out=cw[:, :, :], in0=rank[:, :, :], scalar=2.0, in1=probn[:, :, :],
                                                   op0=ALU.is_lt, op1=ALU.mult).then_inc(router_step, 1)

            def slot(n, trip):
                s = n % GB
                g = n // GB - 1
                if s == 5 and 0 <= g < G:
                    wait_shared(dve, shared_out, "router", g, 0, trip)
                    nc.vector.tensor_reduce(top[:, :], logit[:, :, :], AX, ALU.max).then_inc(router_step, 1)
                    wait(dve, router_step, 11 * g + 1, 11 / GB, trip)
                    nc.vector.tensor_tensor(shift[:, :, :], logit[:, :, :], top[:, :].unsqueeze(2).broadcast_to([P, 4, E]),
                                            ALU.subtract).then_inc(router_step, 1)
                if 0 <= n < B:
                    wait(dve, scores_ready, n + 1, 1, trip)
                    wait(dve, exp_done, n - 1, 1, trip)
                    nc.vector.tensor_reduce(neg_max[:, n % 2, :], scores[:, :].rearrange("p (c j) -> p c j", c=4),
                                            AX, ALU.max, negate=True).then_inc(max_ready, 1)
                m = n - 1
                if 0 <= m < B:
                    wait(dve, pT_hi_done, m + 1, 1, trip)
                    wait(dve, o_ready, m, 1, trip)
                    nc.vector.tensor_tensor(pT_lo[:, :], pT[:, :], pT_hi[:, :].bitcast(F32),
                                            ALU.subtract).then_inc(pT_lo_done, 1)
                f = expert_of(n)
                if f is not None:
                    wait(dve, hid0_ready, f + 1, 1, trip)
                    wait(dve, got_cw[f % 2], 16 * (f // 2 + 1), 8, trip)
                    wait(dve, hs0_lo_done, f, 1, trip)
                    nc.vector.scalar_tensor_tensor(out=hs[:, 0, :], in0=hid[0][:, :],
                                                   scalar=neg_b1[:, 2 * (f % E):2 * (f % E) + 1],
                                                   in1=cw_all[:, f % 2, :], op0=ALU.max, op1=ALU.mult).then_inc(hs0_done, 1)
                if 0 <= n < B:
                    wait(dve, exp_done, n + 1, 1, trip)
                    wait(dve, probs_ready, n - 1, 1, trip)
                    nc.vector.reciprocal(rsums[:, n % 2, :], sums[:, n % 2, :]).then_inc(rsum_ready, 1)
                read_out(n, "a", trip)
                split_latents(n, s, trip)
                normalise_rows(n, s, trip)
                measure_kv(n, 1, trip)
                router_softmax(n, s, trip)
                router_compare(n, s, trip)
                normalise_kv(n, 0, trip)
                normalise_kv(n, 1, trip)
                normalise_kv(n, 2, trip)
                if f is not None:
                    wait(dve, hs0_hi_done, f + 1, 1, trip)
                    nc.vector.tensor_tensor(hs_lo[:, f % 2, 0, :], hs[:, 0, :], hs_hi[:, f % 2, 0, :].bitcast(F32),
                                            ALU.subtract).then_inc(hs0_lo_done, 1)
                read_out(n, "b", trip)
                if 0 <= m < B:
                    wait(dve, o_hi_done, m + 1, 1, trip)
                    b = m % GB
                    nc.vector.tensor_tensor(oT_lo[:, :, b * L:(b + 1) * L], o[:, :].rearrange("p (h i) -> p h i", h=H),
                                            oT_hi[:, :, b * L:(b + 1) * L].bitcast(F32), ALU.subtract).then_inc(o_out, 1)
                split_kv(n, s, trip)
                measure_rows(n, s, trip)
                measure_kv(n, 0, trip)
                aggregate_kv(n, s, trip)
                router_rank(n, s, trip)
                normalise_kv(n, 3, trip)
                read_out(n, "c", trip)

            def read_out(n, place, trip):
                for what, g, number, bank in shared_at(n, place, "dve"):
                    sh = shared[bank]
                    wait_shared(dve, shared_full, what, g, number, trip)
                    if what == "residual":
                        wait_shared(dve, shared_out, "finish", g - 2, 0, trip)
                        wait(dve, got_xres, 16 * (g + 1), 16 / GB, trip)
                        nc.vector.tensor_tensor(x1[:, g % 2, :, :], sh[:, :].rearrange("p (c d) -> p c d", c=4),
                                                xres[:, :, :], ALU.add).then_inc(shared_out[bank], 1)
                    elif what == "finish":
                        wait_shared(dve, shared_full, "turn_x", g + 1, 0, trip)
                        nc.vector.scalar_tensor_tensor(out=res[:, :, :], in0=sh[:, :].rearrange("p (c d) -> p c d", c=4),
                                                       scalar=tg[:, 1:2], in1=x1[:, g % 2, :, :],
                                                       op0=ALU.mult, op1=ALU.add).then_inc(shared_out[bank], 1)
                    elif what == "router":
                        nc.vector.tensor_tensor(logit[:, :, :], sh[:, 0:4 * E].rearrange("p (c e) -> p c e", c=4),
                                                br_all[:, :].unsqueeze(1).broadcast_to([P, 4, E]),
                                                ALU.add).then_inc(shared_out[bank], 1)
                for what, g, number, bank in shared_at(n, place, "act"):
                    if what == "turn_x":
                        wait(dve, xT_hi_done, g + 1, 1 / GB, trip)
                        wait(dve, hid1_ready, E * (g - 1), 1, trip)
                        nc.vector.tensor_tensor(xT_lo[:, g % 2, :], shared[bank][:, :], xT_hi[:, g % 2, :].bitcast(F32),
                                                ALU.subtract).then_inc(shared_out[bank], 1)

            slots(dve, slot, weights)

        @block.tensor
        def _(pe):
            def three_passes(bank, w_hi_, w_lo_, m_hi, m_lo, start=True, stop=True):
                nc.tensor.matmul(bank, w_hi_, m_hi, start=start, stop=False)
                nc.tensor.matmul(bank, w_hi_, m_lo, start=False, stop=False)
                return nc.tensor.matmul(bank, w_lo_, m_hi, start=False, stop=stop)

            def turn_weights(h):
                if h >= 2:
                    pe.wait_ge(w_copied, h - 1)
                for k, w in enumerate((Wq_in[:, h * D:(h + 1) * D], Wkv_in[:, h * D:(h + 1) * D],
                                       Wkv_in[:, (H + h) * D:(H + h + 1) * D])):
                    last = nc.tensor.transpose(hid[h % 2][:, k * P:(k + 1) * P], w, ident[:, :])
                last.then_inc(w_turned, 1)

            def weights(n):
                if n == FOLD_FROM:
                    pe.wait_ge(got_rows, 16 * 4)
                    pe.wait_ge(const_step, 10)
                    nc.tensor.transpose(acc[:, 0:NR], rows[:, :], ident[0:NR, 0:NR]).then_inc(cols_turned, 1)
                    pe.wait_ge(got_attn_w[0], 16 * 3)
                    turn_weights(0)
                    pe.wait_ge(cols_ready, 1)
                for h in FOLD.get(n, ()):
                    if h + 1 == H // 2:
                        pe.wait_ge(got_attn_w[1], 16 * 3)
                    if h + 1 < H:
                        turn_weights(h + 1)
                    fold = [pT, o][h % 2]
                    if h >= 2:
                        pe.wait_ge(w_lo, h - 1)
                    pe.wait_ge(w_copied, h + 1)
                    WqT, WkT, WvT = (wT[:, h % 2, k * P:(k + 1) * P] for k in range(3))
                    nc.tensor.matmul(fold[:, 0:D], WqT, WkT, start=True, stop=True)
                    nc.tensor.matmul(fold[:, D:2 * D], WvT, Wo_in[:, h, :], start=True, stop=True)
                    nc.tensor.matmul(fold[:, 2 * D:2 * D + 1], WkT, cols[:, h:h + 1], start=True, stop=True).then_inc(w_folded, 1)
                if n == FOLD_BIAS:
                    for h in range(H):
                        last = nc.tensor.matmul(acc[:, NR:NR + 1], Wo_in[:, h, :], cols[:, H + h:H + h + 1],
                                                start=(h == 0), stop=(h == H - 1))
                    last.then_inc(bias_folded, 1)
                if n == FOLD_B1 + 1:
                    pe.wait_ge(diag_ready, 2)
                    pe.wait_ge(got_ffn_w, 16 * 3)
                    for e in range(E):
                        last = nc.tensor.matmul(hid[1][0:E, 0:D], b1_diag[:, e, :], W2_in[:, 2 * e * D:(2 * e + 1) * D],
                                                start=(e == 0), stop=(e == E - 1))
                    last.then_inc(bias_folded, 1)

            def slot(n, trip):
                if 0 <= n < B:
                    g, b = n // GB, n % GB
                    if b == 0:
                        wait_shared(pe, shared_out, "query", g, 7, trip)
                    wait(pe, exp_done, n, 1, trip)
                    for c in range(4):
                        last = nc.tensor.matmul(scores[:, c * P:(c + 1) * P],
                                                qT[:, g % 2, b, 2 * c:2 * c + 2, :].rearrange("p h i -> p (h i)"),
                                                kvT[:, g % 2, b, :], start=True, stop=True)
                    last.then_inc(scores_ready, 1)
                m = n - 1
                if 0 <= m < B:
                    wait(pe, probs_ready, m + 1, 1, trip)
                    wait(pe, pT_lo_done, m, 1, trip)
                    for c in range(4):
                        last = nc.tensor.transpose(pT[:, c * P:(c + 1) * P], probs[:, m % 2, c * P:(c + 1) * P], ident[:, :])
                    last.then_inc(pT_ready, 1)
                use_shared(n, "a", trip)
                f = expert_of(n)
                if f is not None:
                    g, e = f // E, f % E
                    if f == 0:
                        pe.wait_ge(ffn_ready, E)
                        pe.wait_ge(bias_ready, 3)
                    if e == 0:
                        wait_shared(pe, shared_out, "turn_x", g, 0, trip)
                    for c, (done, ready) in enumerate(((hs0_done, hid0_ready), (relu_done, hid1_ready))):
                        wait(pe, done, f, 1, trip)
                        three_passes(hid[c][:, :], W1_hi[:, e, c, :], W1_lo[:, e, c, :],
                                     xT_hi[:, g % 2, :], xT_lo[:, g % 2, :]).then_inc(ready, 1)
                use_shared(n, "b", trip)
                if 0 <= m < B:
                    wait(pe, pT_lo_done, m + 1, 1, trip)
                    wait(pe, kv_lo_done, m // GB + 1, 1 / GB, trip)
                    wait(pe, o_out, m, 1, trip)
                    g, b = m // GB, m % GB
                    three_passes(o[:, :], kv_hi[:, g % 2, b, :], kv_lo[:, g % 2, b, :],
                                 pT_hi[:, :], pT_lo[:, :]).then_inc(o_ready, 1)
                f = expert_of(n - 1)
                if f is not None:
                    g, e = f // E, f % E
                    if e == 0:
                        wait(pe, f_done, g, 1 / GB, trip)
                        wait_shared(pe, shared_out, "turn_cw", g, 0, trip)
                        nc.tensor.matmul(acc[:, :], B2[:, :], cwT[:, :], start=True, stop=False)
                    for c, ready in enumerate((hs0_lo_done, hs1_lo_done)):
                        wait(pe, ready, f + 1, 1, trip)
                        last = three_passes(acc[:, :], W2_hi[:, e, c, :], W2_lo[:, e, c, :], hs_hi[:, f % 2, c, :],
                                            hs_lo[:, f % 2, c, :], start=False, stop=(e == E - 1 and c == 1))
                    last.then_inc(ffn_done, 1)
                use_shared(n, "c", trip)

            def use_shared(n, place, trip):
                for what, g, number, places, bank, count in uses[n]:
                    if place not in places:
                        continue
                    sh = shared[bank]
                    if count > 0 and place == places[0]:
                        pe.wait_ge(shared_out[bank], count + trip * shared_per_trip)
                    if what == "turn_kv":
                        wait(pe, kv_ready, 4 * g + 2 * number + 2, 4 / GB, trip)
                        for i in range(4):
                            last = nc.tensor.transpose(sh[:, i * P:(i + 1) * P], kv[:, 4 * number + i, :], ident[:, :])
                    elif what == "query":
                        if g == 0:
                            pe.wait_ge(w_lo, number + 1)
                        if number == 0:
                            wait(pe, latT_done, 2 * (g + 1), 2 / GB, trip)
                        last = three_passes(sh[:, :].rearrange("p (b i) -> p b i", b=GB), AM_hi[:, number, 0, :],
                                            AM_lo[:, number, 0, :], latT_hi[:, :, :], latT_lo[:, :, :])
                    elif what == "project":
                        if place == places[0]:
                            wait(pe, o_out, GB * (g + 1), 1, trip)
                        part, each = places.index(place), H // len(places)
                        for h in range(part * each, (part + 1) * each):
                            last = three_passes(sh[:, :], AM_hi[:, h, 1, :], AM_lo[:, h, 1, :], oT_hi[:, h, :], oT_lo[:, h, :],
                                                start=(h == 0), stop=(h == H - 1))
                    elif what == "residual":
                        wait_shared(pe, shared_out, "project", g, 0, trip)
                        for c in range(4):
                            last = nc.tensor.transpose(sh[:, c * P:(c + 1) * P], yT[:, c * P:(c + 1) * P], ident[:, :])
                    elif what == "turn_x":
                        wait(pe, xn_done, g + 1, 1 / GB, trip)
                        for c in range(4):
                            last = nc.tensor.transpose(sh[:, c * P:(c + 1) * P], xn[:, c, :], ident[:, :])
                    elif what == "router":
                        if g == 0:
                            pe.wait_ge(wr_ready, 1)
                        wait_shared(pe, shared_out, "turn_x", g, 0, trip)
                        for c in range(4):
                            rows_c = slice(c * P, (c + 1) * P)
                            last = three_passes(sh[:, c * E:(c + 1) * E], xT_hi[:, g % 2, rows_c], xT_lo[:, g % 2, rows_c],
                                                Wr_hi[:, :], Wr_lo[:, :])
                    elif what == "turn_cw":
                        wait(pe, router_step, 11 * (g + 1), 11 / GB, trip)
                        for c in range(4):
                            last = nc.tensor.transpose(sh[0:E, c * P:(c + 1) * P], cw[:, c, :], ident[:, :])
                    elif what == "finish":
                        wait(pe, f_done, g + 1, 1 / GB, trip)
                        for c in range(4):
                            last = nc.tensor.transpose(sh[:, c * P:(c + 1) * P], fT[:, c * P:(c + 1) * P], ident[:, :])
                    if place == places[-1]:
                        last.then_inc(shared_full[bank], 1)

            slots(pe, slot, weights)


_INS = ['x', 'ctx_1024', 'g_xattn', 'g_ffn', 'L0_xattn_gamma_media', 'L0_xattn_beta_media', 'L0_xattn_gamma_lat',
        'L0_xattn_beta_lat', 'L0_xattn_Wq', 'L0_xattn_bq', 'L0_xattn_Wkv', 'L0_xattn_bkv', 'L0_xattn_Wo',
        'L0_xattn_bo', 'L0_ffn_Wr', 'L0_ffn_br', 'L0_ffn_W1', 'L0_ffn_b1', 'L0_ffn_W2', 'L0_ffn_b2']
_OUTS = [((B, L, D), 'float32')]


def kernel(**inputs):
    import numpy as _np
    import concourse.bacc as _bacc
    from concourse import mybir as _mybir
    from concourse.bass_utils import run_bass_kernel_spmd as _run

    nc = _bacc.Bacc("TRN2", target_bir_lowering=False, num_devices=1)
    arrays, args = {}, []
    for name in _INS:
        a = _np.ascontiguousarray(inputs[name])
        arrays[f"in_{name}_dram"] = a
        args.append(nc.dram_tensor(f"in_{name}_dram", a.shape, _mybir.dt.from_np(a.dtype), kind="ExternalInput").ap())
    for i, (shape, dtype) in enumerate(_OUTS):
        dt = _mybir.dt.from_np(_np.dtype(dtype))
        args.append(nc.dram_tensor(f"out_{i}_dram", shape, dt, kind="ExternalOutput").ap())
    flamingo(nc, *args)
    r = _run(nc, [arrays], core_ids=[0])
    got = tuple(r.results[0][f"out_{i}_dram"] for i in range(len(_OUTS)))
    return got[0]
```
